# Optimizing a Trainium2 kernel written in Bass

```python
import numpy as np
import jax
import jax.numpy as jnp

def _softmax(x, axis=-1):
    return jax.nn.softmax(x, axis=axis)

def _gelu(x):
    return jax.nn.gelu(x, approximate=True)

def _silu(x):
    return jax.nn.silu(x)

def _sigmoid(x):
    return jax.nn.sigmoid(x)

def _layernorm(x, axis=-1, eps=1e-05):
    m = jnp.mean(x, axis=axis, keepdims=True)
    v = jnp.var(x, axis=axis, keepdims=True)
    return (x - m) / jnp.sqrt(v + eps)

def _scatter_add(tgt, idx, src, axis=0):
    return tgt.at[idx].add(src)

def _segment_sum(src, seg, n):
    return jax.ops.segment_sum(src, seg, n)
kernel_name = 'mk_prb_d1_jaxref_r8_d6e8ae'

def setup_inputs(seed: int=0):
    np.random.seed(seed)
    _w = jnp.asarray

    def _L0_attn_setup():
        import jax, jax.numpy as jnp
        import numpy as np
        B, T, E = (4, 256, 128)
        NUM_HEADS = 16
        HEAD_SIZE = E // NUM_HEADS

        def _rope_tables(T, E):
            thetas = 10000.0 ** (-jnp.arange(0, E, 2, dtype=jnp.float32) / E)
            thetas = jnp.repeat(thetas, 2)
            angles = jnp.arange(T, dtype=jnp.float32)[:, None] * thetas[None, :]
            return (jnp.sin(angles), jnp.cos(angles))

        def _rotate(x, sin, cos):
            Bx, Tx, Ex = x.shape
            xp = x.reshape(Bx, Tx, Ex // 2, 2)
            rot = jnp.stack([-xp[..., 1], xp[..., 0]], axis=-1).reshape(Bx, Tx, Ex)
            return x * cos + rot * sin
        key = jax.random.key(seed)
        ks = jax.random.split(key, 6)
        scale = 1.0 / np.sqrt(E)
        return {'input': jax.random.normal(ks[0], (B, T, E), dtype=jnp.float32), 'Wq': jax.random.normal(ks[1], (E, E), dtype=jnp.float32) * scale, 'Wk': jax.random.normal(ks[2], (E, E), dtype=jnp.float32) * scale, 'Wv': jax.random.normal(ks[3], (E, E), dtype=jnp.float32) * scale, 'Wo': jax.random.normal(ks[4], (E, E), dtype=jnp.float32) * scale, 'bo': jnp.zeros((E,), dtype=jnp.float32)}
    _L0_attn_in = _L0_attn_setup()

    def _L0_ffn_setup():
        import jax, jax.numpy as jnp
        import numpy as np
        DIM = 128
        DEPTH = 2
        HEADS = 8
        DIM_HEAD = 64
        WINDOW = 64
        INNER = HEADS * DIM_HEAD
        HID = int(DIM * 4 * 2 / 3)
        B, N = (2, 1024)
        QK_SCALE = 8.0

        def shift_token(t):
            t1, t2 = jnp.split(t, 2, axis=-1)
            t2 = jnp.pad(t2, ((0, 0), (1, 0), (0, 0)))[:, :-1]
            return jnp.concatenate([t1, t2], axis=-1)

        def l2norm(t):
            return t / jnp.clip(jnp.linalg.norm(t, axis=-1, keepdims=True), 1e-12)

        def rotate_half(x):
            x1, x2 = jnp.split(x, 2, axis=-1)
            return jnp.concatenate([-x2, x1], axis=-1)

        def rotary_xpos(q, k):
            n = q.shape[-2]
            half_idx = jnp.arange(0, DIM_HEAD, 2, dtype=jnp.float32)
            inv_freq = 1.0 / 10000.0 ** (half_idx / DIM_HEAD)
            t = jnp.arange(n, dtype=jnp.float32)
            freqs = t[:, None] * inv_freq[None, :]
            freqs = jnp.concatenate([freqs, freqs], axis=-1)
            base = (half_idx + 0.4 * DIM_HEAD) / (1.4 * DIM_HEAD)
            power = (t - n // 2) / float(WINDOW // 2)
            scale = base[None, :] ** power[:, None]
            scale = jnp.concatenate([scale, scale], axis=-1)
            cos, sin = (jnp.cos(freqs), jnp.sin(freqs))
            q = q * cos * scale + rotate_half(q) * sin * scale
            k = k * cos / scale + rotate_half(k) * sin / scale
            return (q, k)

        def local_attention(q, k, v):
            b, h, n, d = q.shape
            w = n // WINDOW
            bq = q.reshape(b, h, w, WINDOW, d) * QK_SCALE
            bk = k.reshape(b, h, w, WINDOW, d)
            bv = v.reshape(b, h, w, WINDOW, d)

            def look_around(t):
                p = jnp.pad(t, ((0, 0), (0, 0), (1, 0), (0, 0), (0, 0)))
                return jnp.concatenate([p[:, :, :w], p[:, :, 1:]], axis=3)
            bk, bv = (look_around(bk), look_around(bv))
            bt = jnp.arange(n).reshape(w, WINDOW)
            btp = jnp.pad(bt, ((1, 0), (0, 0)), constant_values=-1)
            btk = jnp.concatenate([btp[:w], btp[1:]], axis=1)
            sim = jnp.einsum('bhwid,bhwjd->bhwij', bq, bk)
            i = bt[:, :, None]
            j = btk[:, None, :]
            mask = (i < j) | (i > j + WINDOW) | (j == -1)
            sim = jnp.where(mask, -jnp.finfo(sim.dtype).max, sim)
            attn = jax.nn.softmax(sim, axis=-1)
            out = jnp.einsum('bhwij,bhwjd->bhwid', attn, bv)
            return out.reshape(b, h, n, d)

        def _layer(x, wqkv, qs, ksc, wo, lg, lb, w1, b1, w2, b2):
            b, n, _ = x.shape
            h = shift_token(x)
            qkv = h @ wqkv
            q, k, v = jnp.split(qkv, 3, axis=-1)
            to_heads = lambda t: t.reshape(b, n, HEADS, DIM_HEAD).transpose(0, 2, 1, 3)
            q, k, v = (to_heads(q), to_heads(k), to_heads(v))
            q = l2norm(q) * qs
            k = l2norm(k) * ksc
            q, k = rotary_xpos(q, k)
            o = local_attention(q, k, v)
            o = o.transpose(0, 2, 1, 3).reshape(b, n, INNER)
            x = x + o @ wo
            h = shift_token(x)
            mu = h.mean(-1, keepdims=True)
            var = h.var(-1, keepdims=True)
            h = (h - mu) / jnp.sqrt(var + 1e-05) * lg + lb
            h = h @ w1 + b1
            a, g = jnp.split(h, 2, axis=-1)
            h = a * jax.nn.gelu(g, approximate=False)
            x = x + h @ w2 + b2
            return x
        key = jax.random.key(seed)
        ks = jax.random.split(key, 6)
        return {'x': jax.random.normal(ks[0], (B, N, DIM), jnp.float32), 'wqkv': jax.random.normal(ks[1], (DEPTH, DIM, 3 * INNER), jnp.float32) * 0.02, 'q_scale': jnp.ones((DEPTH, DIM_HEAD), jnp.float32), 'k_scale': jnp.ones((DEPTH, DIM_HEAD), jnp.float32), 'wo': jax.random.normal(ks[2], (DEPTH, INNER, DIM), jnp.float32) * 0.02, 'ln_g': jnp.ones((DEPTH, DIM), jnp.float32), 'ln_b': jnp.zeros((DEPTH, DIM), jnp.float32), 'w1': jax.random.normal(ks[3], (DEPTH, DIM, 2 * HID), jnp.float32) * 0.02, 'b1': jnp.zeros((DEPTH, 2 * HID), jnp.float32), 'w2': jax.random.normal(ks[4], (DEPTH, HID, DIM), jnp.float32) * 0.02, 'b2': jnp.zeros((DEPTH, DIM), jnp.float32)}
    _L0_ffn_in = _L0_ffn_setup()
    _d = {'L0_attn_input': _L0_attn_in['input'], 'L0_attn_Wq': _L0_attn_in['Wq'], 'L0_attn_Wk': _L0_attn_in['Wk'], 'L0_attn_Wv': _L0_attn_in['Wv'], 'L0_attn_Wo': _L0_attn_in['Wo'], 'L0_attn_bo': _L0_attn_in['bo'], 'L0_ffn_wqkv': _L0_ffn_in['wqkv'], 'L0_ffn_q_scale': _L0_ffn_in['q_scale'], 'L0_ffn_k_scale': _L0_ffn_in['k_scale'], 'L0_ffn_wo': _L0_ffn_in['wo'], 'L0_ffn_ln_g': _L0_ffn_in['ln_g'], 'L0_ffn_ln_b': _L0_ffn_in['ln_b'], 'L0_ffn_w1': _L0_ffn_in['w1'], 'L0_ffn_b1': _L0_ffn_in['b1'], 'L0_ffn_w2': _L0_ffn_in['w2'], 'L0_ffn_b2': _L0_ffn_in['b2']}
    _x0 = _d['L0_attn_input']
    _d['L0_attn_input'] = jax.random.normal(jax.random.fold_in(jax.random.key(seed), 1), (16, 256, 128), dtype=_x0.dtype)
    del _x0
    return _d

def reference(L0_attn_input, L0_attn_Wq, L0_attn_Wk, L0_attn_Wv, L0_attn_Wo, L0_attn_bo, L0_ffn_wqkv, L0_ffn_q_scale, L0_ffn_k_scale, L0_ffn_wo, L0_ffn_ln_g, L0_ffn_ln_b, L0_ffn_w1, L0_ffn_b1, L0_ffn_w2, L0_ffn_b2):

    def _L0_attn_ref(input, Wq, Wk, Wv, Wo, bo):
        import jax, jax.numpy as jnp
        import numpy as np
        B, T, E = (4, 256, 128)
        NUM_HEADS = 16
        HEAD_SIZE = E // NUM_HEADS

        def _rope_tables(T, E):
            thetas = 10000.0 ** (-jnp.arange(0, E, 2, dtype=jnp.float32) / E)
            thetas = jnp.repeat(thetas, 2)
            angles = jnp.arange(T, dtype=jnp.float32)[:, None] * thetas[None, :]
            return (jnp.sin(angles), jnp.cos(angles))

        def _rotate(x, sin, cos):
            Bx, Tx, Ex = x.shape
            xp = x.reshape(Bx, Tx, Ex // 2, 2)
            rot = jnp.stack([-xp[..., 1], xp[..., 0]], axis=-1).reshape(Bx, Tx, Ex)
            return x * cos + rot * sin
        Bx, Tx, Ex = input.shape
        sin, cos = _rope_tables(Tx, Ex)
        rx = _rotate(input, sin, cos)
        q = rx @ Wq.T
        k = rx @ Wk.T
        v = input @ Wv.T

        def split_heads(t):
            return t.reshape(Bx, Tx, NUM_HEADS, HEAD_SIZE).transpose(0, 2, 1, 3)
        q, k, v = (split_heads(q), split_heads(k), split_heads(v))
        scores = jnp.einsum('bhqd,bhkd->bhqk', q, k)
        causal = jnp.tril(jnp.ones((Tx, Tx), dtype=bool))
        scores = jnp.where(causal[None, None], scores, -jnp.inf) / np.sqrt(HEAD_SIZE)
        attn = jax.nn.softmax(scores, axis=-1)
        out = jnp.einsum('bhqk,bhkd->bhqd', attn, v)
        out = out.transpose(0, 2, 1, 3).reshape(Bx, Tx, Ex)
        return out @ Wo.T + bo

    def _L0_ffn_ref(x, wqkv, q_scale, k_scale, wo, ln_g, ln_b, w1, b1, w2, b2):
        import jax, jax.numpy as jnp
        import numpy as np
        DIM = 128
        DEPTH = 2
        HEADS = 8
        DIM_HEAD = 64
        WINDOW = 64
        INNER = HEADS * DIM_HEAD
        HID = int(DIM * 4 * 2 / 3)
        B, N = (2, 1024)
        QK_SCALE = 8.0

        def shift_token(t):
            t1, t2 = jnp.split(t, 2, axis=-1)
            t2 = jnp.pad(t2, ((0, 0), (1, 0), (0, 0)))[:, :-1]
            return jnp.concatenate([t1, t2], axis=-1)

        def l2norm(t):
            return t / jnp.clip(jnp.linalg.norm(t, axis=-1, keepdims=True), 1e-12)

        def rotate_half(x):
            x1, x2 = jnp.split(x, 2, axis=-1)
            return jnp.concatenate([-x2, x1], axis=-1)

        def rotary_xpos(q, k):
            n = q.shape[-2]
            half_idx = jnp.arange(0, DIM_HEAD, 2, dtype=jnp.float32)
            inv_freq = 1.0 / 10000.0 ** (half_idx / DIM_HEAD)
            t = jnp.arange(n, dtype=jnp.float32)
            freqs = t[:, None] * inv_freq[None, :]
            freqs = jnp.concatenate([freqs, freqs], axis=-1)
            base = (half_idx + 0.4 * DIM_HEAD) / (1.4 * DIM_HEAD)
            power = (t - n // 2) / float(WINDOW // 2)
            scale = base[None, :] ** power[:, None]
            scale = jnp.concatenate([scale, scale], axis=-1)
            cos, sin = (jnp.cos(freqs), jnp.sin(freqs))
            q = q * cos * scale + rotate_half(q) * sin * scale
            k = k * cos / scale + rotate_half(k) * sin / scale
            return (q, k)

        def local_attention(q, k, v):
            b, h, n, d = q.shape
            w = n // WINDOW
            bq = q.reshape(b, h, w, WINDOW, d) * QK_SCALE
            bk = k.reshape(b, h, w, WINDOW, d)
            bv = v.reshape(b, h, w, WINDOW, d)

            def look_around(t):
                p = jnp.pad(t, ((0, 0), (0, 0), (1, 0), (0, 0), (0, 0)))
                return jnp.concatenate([p[:, :, :w], p[:, :, 1:]], axis=3)
            bk, bv = (look_around(bk), look_around(bv))
            bt = jnp.arange(n).reshape(w, WINDOW)
            btp = jnp.pad(bt, ((1, 0), (0, 0)), constant_values=-1)
            btk = jnp.concatenate([btp[:w], btp[1:]], axis=1)
            sim = jnp.einsum('bhwid,bhwjd->bhwij', bq, bk)
            i = bt[:, :, None]
            j = btk[:, None, :]
            mask = (i < j) | (i > j + WINDOW) | (j == -1)
            sim = jnp.where(mask, -jnp.finfo(sim.dtype).max, sim)
            attn = jax.nn.softmax(sim, axis=-1)
            out = jnp.einsum('bhwij,bhwjd->bhwid', attn, bv)
            return out.reshape(b, h, n, d)

        def _layer(x, wqkv, qs, ksc, wo, lg, lb, w1, b1, w2, b2):
            b, n, _ = x.shape
            h = shift_token(x)
            qkv = h @ wqkv
            q, k, v = jnp.split(qkv, 3, axis=-1)
            to_heads = lambda t: t.reshape(b, n, HEADS, DIM_HEAD).transpose(0, 2, 1, 3)
            q, k, v = (to_heads(q), to_heads(k), to_heads(v))
            q = l2norm(q) * qs
            k = l2norm(k) * ksc
            q, k = rotary_xpos(q, k)
            o = local_attention(q, k, v)
            o = o.transpose(0, 2, 1, 3).reshape(b, n, INNER)
            x = x + o @ wo
            h = shift_token(x)
            mu = h.mean(-1, keepdims=True)
            var = h.var(-1, keepdims=True)
            h = (h - mu) / jnp.sqrt(var + 1e-05) * lg + lb
            h = h @ w1 + b1
            a, g = jnp.split(h, 2, axis=-1)
            h = a * jax.nn.gelu(g, approximate=False)
            x = x + h @ w2 + b2
            return x
        for l in range(DEPTH):
            x = _layer(x, wqkv[l], q_scale[l], k_scale[l], wo[l], ln_g[l], ln_b[l], w1[l], b1[l], w2[l], b2[l])
        return x
    x = L0_attn_input
    xn = _layernorm(x, axis=-1)
    x = x + _L0_attn_ref(xn, L0_attn_Wq, L0_attn_Wk, L0_attn_Wv, L0_attn_Wo, L0_attn_bo) + _L0_ffn_ref(xn, L0_ffn_wqkv, L0_ffn_q_scale, L0_ffn_k_scale, L0_ffn_wo, L0_ffn_ln_g, L0_ffn_ln_b, L0_ffn_w1, L0_ffn_b1, L0_ffn_w2, L0_ffn_b2)
    return x

_drawn_inputs = setup_inputs


def setup_inputs(seed=0):
    import zlib

    import numpy as np

    out = dict(_drawn_inputs(seed))
    spreads = {'L0_attn_bo': (0.0, 0.8),
     'L0_ffn_q_scale': (1.0, 0.6),
     'L0_ffn_k_scale': (1.0, 0.6),
     'L0_ffn_ln_g': (1.0, 0.6),
     'L0_ffn_ln_b': (0.0, 0.8),
     'L0_ffn_b1': (0.0, 0.8),
     'L0_ffn_b2': (0.0, 0.463)}
    factors = {'L0_ffn_wqkv': 3.406,
     'L0_ffn_wo': 3.41,
     'L0_ffn_w1': 6.2,
     'L0_ffn_w2': 6.111,
     'L0_attn_Wq': 4.973,
     'L0_attn_Wk': 4.949,
     'L0_attn_Wv': 3.592,
     'L0_attn_Wo': 3.596}
    for name, (base, spread) in spreads.items():
        noise = np.random.default_rng([zlib.crc32(name.encode()), seed]).standard_normal(out[name].shape)
        drawn = base * np.exp(spread * noise) if base else spread * noise
        out[name] = jnp.asarray(drawn.astype(out[name].dtype))
    for name, factor in factors.items():
        out[name] = (out[name] * factor).astype(out[name].dtype)
    return out
```

```python
from contextlib import ExitStack

import numpy as np
import concourse.bass as bass
from concourse import mybir

ALU = mybir.AluOpType
ACT = mybir.ActivationFunctionType
AX_X = mybir.AxisListType.X
F32 = mybir.dt.float32
BF16 = mybir.dt.bfloat16

P = 128
T = 256
PAIR = 2
TILES = PAIR * T // P
N = PAIR * T
HA, DA = 16, 8
HB, DB = 8, 64
WIN = 64
DEPTH = 2
INNER = HB * DB
CH = INNER // P
HID = 341
HC = [(0, 128), (128, 128), (256, 85)]
NEG = -1.0e30
EPS = 1e-5
LN2 = float(np.log(2.0))


def causal_position(pos):
    return 4 * (pos % 4) + pos // 4


def shape_constants():
    f = np.float32
    t = np.arange(T, dtype=f)
    theta = np.repeat(f(10000.0) ** (-np.arange(0, P, 2, dtype=f) / f(P)), 2).astype(f)
    ang = (t[:, None] * theta[None, :]).astype(f)
    cos_a, sin_a = np.cos(ang), np.sin(ang)
    sin_a[:, 0::2] *= -1
    half = np.arange(0, DB, 2, dtype=f)
    inv = (f(1.0) / f(10000.0) ** (half / f(DB))).astype(f)
    fr = (t[:, None] * inv[None, :]).astype(f)
    fr = np.concatenate([fr, fr], -1)
    base = ((half + f(0.4 * DB)) / f(1.4 * DB)).astype(f)
    sc = base[None, :] ** ((t - T // 2) / f(WIN // 2))[:, None].astype(f)
    sc = np.concatenate([sc, sc], -1).astype(f)
    sign = np.ones(DB, f)
    sign[:DB // 2] = -1
    cos_b = np.stack([np.cos(fr) * sc * 8, np.cos(fr) / sc], 1)
    sin_b = np.stack([np.sin(fr) * sign * sc * 8, np.sin(fr) * sign / sc], 1)
    halves = lambda a: a.reshape(2, P, -1).transpose(1, 0, 2).reshape(P, -1)
    row = np.arange(P)
    head = np.stack([(row // DA == causal_position(p)) / np.sqrt(DA) for p in range(HA)], 1)
    q, k = row[:, None], row[None, :]
    causal = np.where(k <= q, 0, NEG)
    open_ = np.zeros((P, P))
    first = np.where((k <= q) & (k >= q - WIN), 0, NEG)
    k2 = np.arange(WIN, T)[None, :]
    second = np.where((k2 <= q + P) & (k2 >= q + P - WIN), 0, NEG)
    parts = [
        ("ident", np.eye(P)), ("cos_a", halves(cos_a)), ("sin_a", halves(sin_a)),
        ("cos_b", halves(cos_b)), ("sin_b", halves(sin_b)), ("head", head),
        ("mask_a0", np.tile(causal, (1, 4))), ("mask_a1", np.tile(np.concatenate([open_, causal], 1), (1, 2))),
        ("mask_b0", np.tile(first, (1, 4))), ("mask_b1", np.tile(second, (1, 2))),
    ]
    at, n = {}, 0
    for name, a in parts:
        at[name] = (n, n + a.shape[1])
        n += a.shape[1]
    return at, np.ascontiguousarray(np.concatenate([a for _, a in parts], 1).astype(f))


def attention_groups():
    a, b = [], []
    for t in range(TILES):
        heads = 4 if t % 2 == 0 else 2
        for p in range(0, HA, heads):
            a.append(("a", t, p, heads, P * (1 + t % 2), 0))
        for p in range(0, HB, heads):
            b.append(("b", t, p, heads, P if t % 2 == 0 else T - WIN, 0 if t % 2 == 0 else WIN))
    return a, b


A_GROUPS, B_GROUPS = attention_groups()
GROUPS = []


def _schedule():
    out = []
    left = list(A_GROUPS)

    def att(g, layer):
        GROUPS.append((*g, layer))
        out.append(("att", len(GROUPS) - 1))

    def causal(n):
        for _ in range(n):
            if left:
                att(left.pop(0), 0)

    out += [("norm", 0), ("turn_x", 0), ("qkv_a", 0)]
    for layer in range(DEPTH):
        for t in range(TILES):
            out.append(("qkv_b", (layer, t)))
            if t >= 1:
                out.append(("turn_qk", (layer, t - 1)))
            causal(1)
        out.append(("turn_qk", (layer, TILES - 1)))
        for g in B_GROUPS:
            att(g, layer)
        out.append(("drain", 0))
        out.append(("wo", layer))
        causal(2)
        out.append(("mean", layer))
        causal(1)
        out.append(("var", layer))
        causal(2)
        for c in range(len(HC)):
            out.append(("up", (layer, c)))
            causal(1)
        out.append(("down", layer))
        if layer == DEPTH - 1:
            causal(len(left))
            out.append(("drain", 0))
    out.append(("final", 0))
    return out


SCHEDULE = _schedule()
NG = len(GROUPS)


def with_lags(**lags):
    out, last, done = [], -1, {name: 0 for name in lags}
    for item in SCHEDULE:
        if item[0] == "att":
            last = item[1]
            for name, lag in lags.items():
                while done[name] <= last - lag:
                    out.append((name, done[name]))
                    done[name] += 1
        elif item[0] == "drain":
            for name in lags:
                while done[name] <= last:
                    out.append((name, done[name]))
                    done[name] += 1
        else:
            out.append(item)
    return out


PE_ORDER = with_lags(scores=0, turn_p=2, values=3)



def tile_key(k):
    return ("out", GROUPS[k][0], GROUPS[k][6], GROUPS[k][1])


def _tile_groups():
    found = {}
    for k in range(NG):
        found.setdefault(tile_key(k), []).append(k)
    return found


TILE_GROUPS = _tile_groups()


def _bank_turns():
    turn, count = {}, {}

    def use(bank, key):
        turn[key] = (bank, count.get(bank, 0))
        count[bank] = count.get(bank, 0) + 1

    ring = 0
    for name, a in PE_ORDER:
        if name == "scores":
            use(f"scores{a % 2}", ("scores", a))
        elif name == "turn_p":
            use(f"turned{ring % 2}", ("turn_p", a))
            ring += 1
        elif name == "values":
            if TILE_GROUPS[tile_key(a)][0] == a:
                use("out_" + GROUPS[a][0], tile_key(a))
        elif name in ("turn_x", "turn_qk"):
            for part in range(2):
                use(f"turned{ring % 2}", (name, a, part))
                ring += 1
        elif name in ("qkv_a", "qkv_b"):
            use("pair", (name, a))
            use("single", (name + "_v", a))
        elif name == "up":
            use("pair", (name, a))
        elif name in ("wo", "mean", "var", "down", "final"):
            use("single", (name, a))
    return turn, count


TURN, USES = _bank_turns()


def program(nc, x, wq, wk, wv, wo_a, bo, wqkv, qs, ks, wo, lg, lb, w1, b1, w2, b2, consts, out):
    at, _ = shape_constants()
    turns = x.shape[0] // PAIR
    with ExitStack() as ctx:
        def sb(name, shape, dt=F32):
            return ctx.enter_context(nc.sbuf_tensor(name, shape, dt))

        def sem(name):
            return ctx.enter_context(nc.semaphore(name))

        CONST = sb("CONST", [P, consts.shape[1]])
        def table(name):
            return CONST[:, at[name][0]:at[name][1]]
        MASKS = sb("MASKS", [P, at["mask_b1"][1] - at["mask_a0"][0]], BF16)
        def mask(name):
            return MASKS[:, at[name][0] - at["mask_a0"][0]:at[name][1] - at["mask_a0"][0]]
        IDENT = table("ident")
        IDENT_B = sb("IDENT_B", [P, P], BF16)
        MEAN = sb("MEAN", [P, P])
        WA = sb("WA", [P, 4, P])
        WAT = sb("WAT", [P, 4, P])
        WQKV = sb("WQKV", [P, DEPTH, 3 * INNER])
        WO = sb("WO", [P, DEPTH, CH, P])
        W1 = sb("W1", [P, DEPTH, 2 * HID])
        W2 = sb("W2", [P, DEPTH, len(HC), P])
        B1 = sb("B1", [P, DEPTH, 2, len(HC)])
        COLS = sb("COLS", [P, 3, DEPTH])
        BO = sb("BO", [P, P])
        QKS = sb("QKS", [P, DEPTH, 2, DB])
        COS_B = sb("COS_B", [P, DEPTH, 2, 2, DB])
        SIN_B = sb("SIN_B", [P, DEPTH, 2, 2, DB])
        EPSC = sb("EPSC", [P, 1])
        LNB = sb("LNB", [P, 1])
        X = sb("X", [P, TILES, P])
        XR = sb("XR", [P, N])
        XN = sb("XN", [P, TILES, P])
        ROT1 = sb("ROT1", [P, TILES, P])
        ROT2 = sb("ROT2", [P, TILES, P])
        RX = sb("RX", [P, TILES, P])
        STATS = sb("STATS", [P, TILES, 6])
        WAITED = sb("WAITED", [P, 1])
        MV = sb("MV", [P, TILES, 2])
        LNV = sb("LNV", [P, TILES])
        RSTD = sb("RSTD", [P, TILES])
        XT = [sb(f"XT{n}", [P, N]) for n in range(3)]
        H = sb("H", [P, PAIR, T + 1])
        RXT = sb("RXT", [P, N])
        QA = sb("QA", [P, N])
        KA = sb("KA", [P, N])
        KMA = sb("KMA", [P, HA, N])
        VA = sb("VA", [P, TILES, HA * 32])
        OA = sb("OA", [P, N])
        SQ = sb("SQ", [P, 2 * INNER])
        NN = sb("NN", [P, 4, 2 * HB])
        AN = sb("AN", [P, 2 * INNER])
        T1 = sb("T1", [P, 2 * INNER])
        T2 = sb("T2", [P, 2 * INNER])
        QKR = sb("QKR", [P, 2 * INNER])
        QB = sb("QB", [P, CH, N])
        KMB = sb("KMB", [P, CH, 2, N])
        VB = sb("VB", [P, TILES, INNER])
        OB = sb("OB", [P, CH, N])
        PROB = [sb(f"PROB{n}", [P, 512]) for n in range(2)]
        PROB_L = [sb(f"PROB_L{n}", [P, 2, T]) for n in range(2)]
        PT = [sb(f"PT{n}", [P, 512]) for n in range(2)]
        NMAX = sb("NMAX", [P, 2, 4])
        SUM = sb("SUM", [P, 2, 4])
        RSUM = sb("RSUM", [P, 2, 4])
        HCEN = ROT1[:, :, :].rearrange("p t e -> p (t e)")
        HSQ = ROT2[:, :, :].rearrange("p t e -> p (t e)")
        HLN = RXT
        HRS = KA
        HN = RX[:, :, :].rearrange("p t e -> p (t e)")
        HG = sb("HG", [P, N])
        GEL = sb("GEL", [P, N])
        HIDT = sb("HIDT", [P, len(HC), N])
        OUT = sb("OUT", [P, TILES, P])

        bank = {name: ctx.enter_context(nc.psum_tensor("ps_" + name, [P, w], F32)) for name, w in
                (("scores0", 512), ("scores1", 512), ("turned0", 512), ("turned1", 512), ("pair", 1024),
                 ("single", 512), ("out", 512))}
        bank["out_a"] = bank["out"]
        bank["out_b"] = bank["out"]

        names = ("scores0", "scores1", "turned0", "turned1", "pair", "single", "out")
        filled = {n: sem("filled_" + n) for n in names}
        emptied = {n: sem("emptied_" + n) for n in names}

        s_load, s_weights, s_store = sem("x_loaded"), sem("weights_loaded"), sem("out_stored")
        s_ones, s_masks, s_wat, s_wturn = sem("constants_ready"), sem("masks_ready"), sem("wat_ready"), sem("w_turned")
        s_tab = sem("tables_ready")
        s_mv, s_lnv, s_rstd, s_xn = sem("mv_ready"), sem("lnv_ready"), sem("rstd_ready"), sem("xn_ready")
        s_stats = sem("stats_ready")
        s_rot, s_rx, s_xr = sem("rot_ready"), sem("rx_ready"), sem("xr_ready")
        s_h, s_rxt = sem("h_ready"), sem("rxt_ready")
        s_qa, s_kma, s_va = sem("qa_ready"), sem("kma_ready"), sem("va_ready")
        s_sq, s_n2r, s_n2, s_ln, s_rn, s_an = (sem(n) for n in ("sq_ready", "n2_raw", "n2_ready", "n2_ln", "rn_ready", "an_ready"))
        s_t1, s_t2, s_qkr = sem("t1_ready"), sem("t2_ready"), sem("qkr_ready")
        s_qb, s_kmb, s_vb = sem("qb_ready"), sem("kmb_ready"), sem("vb_ready")
        s_max, s_exp, s_rs, s_prob, s_pt, s_pv = (sem(n) for n in ("max_ready", "exp_ready", "rsum_ready", "prob_ready", "pt_ready", "pt_used"))
        s_tp = sem("prob_used")
        s_oa, s_ob = sem("oa_ready"), sem("ob_ready")
        s_x1, s_h2, s_cen, s_hsq, s_hln, s_hrs, s_hn, s_hg = (sem(n) for n in (
            "x1_ready", "h2_ready", "centred", "hsq_ready", "hln_ready", "hrs_ready", "hn_ready", "hg_ready"))
        s_gel, s_hid, s_x2, s_out = sem("gelu_ready"), sem("hidden_ready"), sem("x2_ready"), sem("out_ready")

        block = ctx.enter_context(nc.Block())
        x_view = x.rearrange("(i b) (h p) e -> i p (b h) e", b=PAIR, p=P)
        out_view = out.rearrange("(i b) (h p) e -> i p (b h) e", b=PAIR, p=P)
        WEIGHT_LOADS = [0]

        def bank_name(key):
            b = TURN[key][0]
            return "out" if b.startswith("out") else b

        order, per = {}, {n: 0 for n in names}
        for key, (b, _) in TURN.items():
            n = bank_name(key)
            order[key] = per[n]
            per[n] += 1

        def take(e, i, key):
            n = bank_name(key)
            e.wait_ge(emptied[n], i * per[n] + order[key] + 1)
            return bank[n]

        def full(e, i, key):
            n = bank_name(key)
            e.wait_ge(filled[n], i * per[n] + order[key] + 1)
            return bank[n]

        def taken(e, i, key):
            n = bank_name(key)
            e.wait_ge(emptied[n], i * per[n] + order[key] + 2)

        def turn_before(e, i):
            e.wait_ge(emptied["single"], i * per["single"] + 1)

        def tile_tokens(t):
            return slice(t * P, (t + 1) * P)

        def probs(k):
            kind, t, p0, heads, keys, k0, layer = GROUPS[k]
            if kind == "b" and t % 2 == 1:
                return PROB_L[k % 2][:, :, k0:k0 + keys]
            return PROB[k % 2][:, 0:heads * keys].rearrange("p (h k) -> p h k", h=heads)

        def prob_block(k, h, kb):
            kind, t, p0, heads, keys, k0, layer = GROUPS[k]
            if kind == "b" and t % 2 == 1:
                return PROB_L[k % 2][:, h, kb * P:(kb + 1) * P]
            return PROB[k % 2][:, h * keys + kb * P:h * keys + (kb + 1) * P]

        def evac_engine(k):
            return "act" if k % 4 == 0 else "dve"

        def evac(e, i, k):
            b = full(e, i, ("turn_p", k))
            if k >= 2:
                e.wait_ge(s_pv, i * NG + k - 1)
            kind, t, p0, heads, keys, k0, layer = GROUPS[k]
            done = emptied[bank_name(("turn_p", k))]
            if e.engine == mybir.EngineType.Activation:
                e.activation(PT[k % 2][:, :], b[:, :], ACT.Copy).then_inc(done, 1)
            else:
                e.tensor_copy(PT[k % 2][:, :], b[:, :]).then_inc(done, 1)

        @block.sync
        def _(sp):
            def load(dst, src):
                sp.dma_start(dst, src).then_inc(s_weights, 16)
                WEIGHT_LOADS[0] += 1
            sp.dma_start(CONST[:, :], consts).then_inc(s_weights, 16)
            WEIGHT_LOADS[0] += 1
            for n, w in enumerate((wq, wk, wv, wo_a)):
                load(WA[:, n, :], w)
            load(BO[:, :], bo.rearrange("(a n) -> a n", a=1).to_broadcast([P, P]))
            for layer in range(DEPTH):
                load(QKS[:, layer, 0, :], qs[layer:layer + 1, :].to_broadcast([P, DB]))
                load(QKS[:, layer, 1, :], ks[layer:layer + 1, :].to_broadcast([P, DB]))
                load(WQKV[:, layer, :], wqkv[layer])
                load(WO[:, layer, :, :], wo[layer].rearrange("(c p) n -> p c n", p=P))
                load(W1[:, layer, :], w1[layer])
                for c, (a, m) in enumerate(HC):
                    load(W2[0:m, layer, c, :], w2[layer, a:a + m, :])
                    for g in range(2):
                        load(B1[0:m, layer, g, c:c + 1], b1[layer, g * HID + a:g * HID + a + m].rearrange("(p a) -> p a", a=1))
                for n, v in enumerate((lg, lb, b2)):
                    load(COLS[:, n, layer:layer + 1], v[layer].rearrange("(p a) -> p a", a=1))
            sp.dma_start(X[:, :, :], x_view[0]).then_inc(s_load, 16)
            with sp.Fori(1, turns) as i:
                sp.wait_ge(s_xn, i * TILES)
                sp.wait_ge(s_xr, i)
                sp.dma_start(X[:, :, :], x_view[i]).then_inc(s_load, 16)

        NW = WEIGHT_LOADS

        @block.gpsimd
        def _(pool):
            for n in names:
                pool.sem_inc(emptied[n], 1)
            pool.sem_inc(s_store, 1)
            pool.memset(MEAN[:, :], 1.0 / P).then_inc(s_ones, 1)
            pool.memset(EPSC[:, :], EPS).then_inc(s_ones, 1)
            pool.memset(LNB[:, :], 10 * LN2).then_inc(s_ones, 1)
            pool.memset(H[:, :, :], 0.0).then_inc(s_ones, 1)
            pool.memset(KMB[:, :, :, :], 0.0).then_inc(s_ones, 1)
            pool.memset(VA[:, :, :], 0.0).then_inc(s_ones, 1)
            pool.memset(PROB_L[0][:, :, :], 0.0).then_inc(s_ones, 1)
            pool.memset(PROB_L[1][:, :, :], 0.0).then_inc(s_ones, 1)
            pool.wait_ge(s_weights, 16 * NW[0])
            with pool.Fori(0, turns) as i:
                for name, a in with_lags(norm_p=0):
                    if name == "norm":
                        pool.wait_ge(s_load, 16 * i + 16)
                        turn_before(pool, i)
                        pool.tensor_tensor(XR[:, :].rearrange("p (t e) -> p t e", e=P), X[:, :, :],
                                           BO[:, None, :].to_broadcast([P, TILES, P]), ALU.add).then_inc(s_xr, 1)
                        pool.wait_ge(s_xn, i * TILES + TILES)
                        for u in range(PAIR):
                            r1 = ROT1[:, 2 * u:2 * u + 2, :]
                            xn = XN[:, 2 * u:2 * u + 2, :]
                            cos = table("cos_a").rearrange("p (h e) -> p h e", e=P)
                            sin = table("sin_a").rearrange("p (h e) -> p h e", e=P)
                            pool.tensor_tensor(r1, xn, cos, ALU.mult).then_inc(s_rot, 1)
                            for odd in range(2):
                                pool.tensor_tensor(ROT2[:, 2 * u:2 * u + 2, odd::2], xn[:, :, 1 - odd::2],
                                                   sin[:, :, odd::2], ALU.mult).then_inc(s_rot, 1)
                        pool.wait_ge(s_rot, i * 6 + 6)
                        pool.tensor_tensor(RX[:, :, :], ROT1[:, :, :], ROT2[:, :, :], ALU.add).then_inc(s_rx, 1)
                    elif name == "qkv_b":
                        layer, t = a
                        n = layer * TILES + t
                        taken(pool, i, ("qkv_b", a))
                        pool.tensor_tensor(T1[:, :].rearrange("p (s h d) -> p s h d", s=2, d=DB),
                                           AN[:, :].rearrange("p (s h d) -> p s h d", s=2, d=DB),
                                           COS_B[:, layer, t % 2, :, None, :].to_broadcast([P, 2, HB, DB]),
                                           ALU.mult).then_inc(s_t1, 1)
                        pool.wait_ge(s_t1, i * 8 + n + 1)
                        pool.wait_ge(s_t2, i * 16 + 2 * n + 2)
                        if n == 0:
                            turn_before(pool, i)
                        else:
                            pl, pt = (n - 1) // TILES, (n - 1) % TILES
                            full(pool, i, ("turn_qk", (pl, pt), 1))
                        pool.tensor_tensor(QKR[:, :], T1[:, :], T2[:, :], ALU.add).then_inc(s_qkr, 1)
                    elif name == "norm_p":
                        kind, t, p0, heads, keys, k0, layer = GROUPS[a]
                        pool.wait_ge(s_rs, i * NG + a + 1)
                        v = probs(a)
                        pool.tensor_tensor(v, v, RSUM[:, a % 2, 0:heads, None].to_broadcast([P, heads, keys]),
                                           ALU.mult).then_inc(s_prob, 1)

        @block.scalar
        def _(act):
            act.wait_ge(s_weights, 16 * NW[0])
            act.wait_ge(s_ones, 8)
            with act.Fori(0, turns) as i:
                for name, a in with_lags(exp=0, evac=2):
                    if name == "norm":
                        act.wait_ge(s_mv, i * TILES + TILES)
                        act.activation(LNV[:, :], MV[:, :, 1], ACT.Ln, bias=EPSC[:, 0:1]).then_inc(s_lnv, 1)
                        act.wait_ge(s_lnv, i + 1)
                        act.activation(RSTD[:, :], LNV[:, :], ACT.Exp, scale=-0.5).then_inc(s_rstd, 1)
                    elif name == "turn_x":
                        b = full(act, i, ("turn_x", 0, 0))
                        turn_before(act, i)
                        act.activation(XT[0][:, :], b[:, :], ACT.Copy).then_inc(s_h, 1)
                        bt = b[:, :].rearrange("p (u t) -> p u t", u=PAIR)
                        act.activation(H[0:64, :, 0:T], bt[0:64], ACT.Copy).then_inc(s_h, 1)
                        act.activation(H[64:P, :, 1:T + 1], bt[64:P], ACT.Copy).then_inc(emptied[bank_name(("turn_x", 0, 0))], 1)
                    elif name == "qkv_a":
                        b = full(act, i, ("qkv_a", 0))
                        act.activation(QA[:, :], b[:, 0:N], ACT.Copy).then_inc(s_qa, 1)
                        act.activation(KA[:, :], b[:, N:2 * N], ACT.Copy).then_inc(emptied["pair"], 1)
                    elif name == "qkv_b":
                        layer, t = a
                        n = layer * TILES + t
                        b = full(act, i, ("qkv_b", a))
                        act.activation(SQ[:, :], b[:, :], ACT.Square).then_inc(s_sq, 1)
                        b = full(act, i, ("qkv_b_v", a))
                        act.activation(VB[:, t, :], b[:, :], ACT.Copy).then_inc(emptied["single"], 1)
                        act.wait_ge(s_n2, i * 8 + n + 1)
                        act.activation(NN[:, 2, :], NN[:, 1, :], ACT.Ln, scale=float(2 ** 20)).then_inc(s_ln, 1)
                        act.wait_ge(s_ln, i * 8 + n + 1)
                        act.activation(NN[:, 3, :], NN[:, 2, :], ACT.Exp, bias=LNB[:, 0:1], scale=-0.5).then_inc(s_rn, 1)
                    elif name == "turn_qk":
                        layer, t = a
                        b = full(act, i, ("turn_qk", a, 0))
                        act.activation(QB[:, :, tile_tokens(t)], b[:, :].rearrange("p (c q) -> p c q", c=CH),
                                       ACT.Copy).then_inc(emptied[bank_name(("turn_qk", a, 0))], 1)
                    elif name == "exp":
                        kind, t, p0, heads, keys, k0, layer = GROUPS[a]
                        act.wait_ge(s_max, i * NG + a + 1)
                        if a >= 2:
                            full(act, i, ("turn_p", a - 2))
                        b = bank[f"scores{a % 2}"]
                        v = probs(a)
                        for h in range(heads):
                            ins = act.activation(v[:, h, :], b[:, h * keys:(h + 1) * keys], ACT.Exp,
                                                 bias=NMAX[:, a % 2, h:h + 1], accum_out=SUM[:, a % 2, h:h + 1])
                        ins.then_inc(emptied[f"scores{a % 2}"], 1)
                    elif name == "evac":
                        if evac_engine(a) == "act":
                            evac(act, i, a)
                    elif name == "var":
                        taken(act, i, ("mean", a))
                        act.activation(HSQ[:, :], HCEN[:, :], ACT.Square).then_inc(s_hsq, 1)
                        b = full(act, i, ("var", a))
                        act.activation(HLN[:, :], b[:, :], ACT.Ln, bias=EPSC[:, 0:1]).then_inc(emptied["single"], 1)
                        taken(act, i, ("var", a))
                        act.activation(HRS[:, :], HLN[:, :], ACT.Exp, scale=-0.5).then_inc(s_hrs, 1)
                    elif name == "up":
                        layer, c = a
                        m = HC[c][1]
                        n = layer * len(HC) + c
                        b = full(act, i, ("up", a))
                        act.activation(GEL[0:m, :], b[0:m, N:2 * N], ACT.Gelu,
                                       bias=B1[0:m, layer, 1, c:c + 1]).then_inc(s_gel, 1)
                taken(act, i, ("final", 0))
                act.dma_start(out_view[i], OUT[:, :, :]).then_inc(s_store, 16)
            act.wait_ge(s_store, 16 * turns + 1)

        @block.vector
        def _(dve):
            def shift(src, done):
                v = src[:, :].rearrange("p (u t) -> p u t", u=PAIR)
                dve.tensor_copy(H[0:64, :, 0:T], v[0:64])
                dve.tensor_copy(H[64:P, :, 1:T + 1], v[64:P]).then_inc(done, 1)

            dve.wait_ge(s_weights, 16 * NW[0])
            dve.wait_ge(s_ones, 8)
            a0, a1 = at["mask_a0"][0], at["mask_b1"][1]
            dve.tensor_copy(MASKS[:, :], CONST[:, a0:a1]).then_inc(s_masks, 1)
            dve.tensor_copy(IDENT_B[:, :], IDENT).then_inc(s_masks, 1)
            dve.wait_ge(s_wturn, 1)
            dve.tensor_copy(WAT[:, :, :], bank["turned0"][:, :].rearrange("p (w e) -> p w e", w=4)).then_inc(s_wat, 1)
            for layer in range(DEPTH):
                for hf in range(2):
                    tabs = [table(n).rearrange("p (h s d) -> p h s d", h=2, s=2)[:, hf] for n in ("cos_b", "sin_b")]
                    dve.tensor_tensor(COS_B[:, layer, hf], tabs[0], QKS[:, layer], ALU.mult).then_inc(s_tab, 1)
                    for o in range(2):
                        d, s = slice(32 * o, 32 * o + 32), slice(32 - 32 * o, 64 - 32 * o)
                        dve.tensor_tensor(SIN_B[:, layer, hf, :, d], tabs[1][:, :, d], QKS[:, layer, :, s],
                                          ALU.mult).then_inc(s_tab, 1)
            dve.wait_ge(s_tab, 12)
            with dve.Fori(0, turns) as i:
                for name, a in with_lags(max=0, rsum=1, evac=2, tile=3):
                    if name == "norm":
                        dve.wait_ge(s_load, 16 * i + 16)
                        turn_before(dve, i)
                        for t in range(TILES):
                            dve.bn_stats(STATS[:, t, :], X[:, t, :]).then_inc(s_stats, 1)
                        dve.wait_ge(s_stats, i * TILES + TILES)
                        dve.memset(WAITED[:, :], 0.0)
                        for t in range(TILES):
                            dve.bn_aggr(MV[:, t, :], STATS[:, t, :]).then_inc(s_mv, 1)
                        dve.wait_ge(s_rstd, i + 1)
                        for t in range(TILES):
                            dve.tensor_scalar(XN[:, t, :], X[:, t, :], MV[:, t, 0:1], RSTD[:, t:t + 1],
                                              ALU.subtract, ALU.mult).then_inc(s_xn, 1)
                    elif name == "turn_x":
                        b = full(dve, i, ("turn_x", 0, 1))
                        dve.tensor_copy(RXT[:, :], b[:, :]).then_inc(emptied[bank_name(("turn_x", 0, 1))], 1)
                    elif name == "qkv_a":
                        b = full(dve, i, ("qkv_a_v", 0))
                        for t in range(TILES):
                            va = VA[:, t, :].rearrange("p (j c) -> p j c", j=4)
                            v = b[:, t * P:(t + 1) * P].rearrange("p (j c) -> p j c", j=4)
                            dve.tensor_copy(va[:, :, 0:120].rearrange("p j (q c) -> p j q c", c=40)[:, :, :, 0:DA],
                                            v[:, :, 0:24].rearrange("p j (q c) -> p j q c", c=DA))
                            ins = dve.tensor_copy(va[:, :, 120:128], v[:, :, 24:32])
                        ins.then_inc(emptied["single"], 1)
                        taken(dve, i, ("qkv_a", 0))
                        for p in range(HA):
                            dve.tensor_scalar(KMA[:, p, :], KA[:, :], table("head")[:, p:p + 1], None,
                                              ALU.mult).then_inc(s_kma, 1)
                    elif name == "qkv_b":
                        layer, t = a
                        n = layer * TILES + t
                        dve.wait_ge(s_sq, i * 8 + n + 1)
                        dve.tensor_reduce(NN[:, 0, :], SQ[:, :].rearrange("p (h d) -> p h d", d=DB), AX_X,
                                          ALU.add).then_inc(s_n2r, 1)
                        dve.wait_ge(s_n2r, i * 8 + n + 1)
                        dve.tensor_scalar(NN[:, 1, :], NN[:, 0, :], 1e-24, None, ALU.max).then_inc(s_n2, 1)
                        dve.wait_ge(s_rn, i * 8 + n + 1)
                        if n:
                            dve.wait_ge(s_t1, i * 8 + n)
                        b = bank["pair"]
                        dve.tensor_tensor(AN[:, :].rearrange("p (h d) -> p h d", d=DB),
                                          b[:, :].rearrange("p (h d) -> p h d", d=DB),
                                          NN[:, 3, :, None].to_broadcast([P, 2 * HB, DB]), ALU.mult).then_inc(emptied["pair"], 1)
                        taken(dve, i, ("qkv_b", a))
                        if n:
                            dve.wait_ge(s_qkr, i * 8 + n)
                        an = AN[:, :].rearrange("p (s h d) -> p s h d", s=2, d=DB)
                        t2 = T2[:, :].rearrange("p (s h d) -> p s h d", s=2, d=DB)
                        for o in range(2):
                            d, s = slice(32 * o, 32 * o + 32), slice(32 - 32 * o, 64 - 32 * o)
                            dve.tensor_tensor(t2[:, :, :, d], an[:, :, :, s],
                                              SIN_B[:, layer, t % 2, :, None, d].to_broadcast([P, 2, HB, 32]),
                                              ALU.mult).then_inc(s_t2, 1)
                    elif name == "turn_qk":
                        layer, t = a
                        b = full(dve, i, ("turn_qk", a, 1))[:, :].rearrange("p (c q) -> p c q", c=CH)
                        dve.tensor_copy(KMB[0:64, :, 0, tile_tokens(t)], b[0:64])
                        dve.tensor_copy(KMB[64:P, :, 1, tile_tokens(t)], b[64:P]).then_inc(
                            emptied[bank_name(("turn_qk", a, 1))], 1)
                    elif name == "max":
                        kind, t, p0, heads, keys, k0, layer = GROUPS[a]
                        b = full(dve, i, ("scores", a))
                        dve.tensor_reduce(NMAX[:, a % 2, 0:heads],
                                          b[:, 0:heads * keys].rearrange("p (h k) -> p h k", h=heads), AX_X,
                                          ALU.max, negate=True).then_inc(s_max, 1)
                    elif name == "rsum":
                        heads = GROUPS[a][3]
                        taken(dve, i, ("scores", a))
                        if a >= 2:
                            dve.wait_ge(s_prob, i * NG + a - 1)
                        dve.reciprocal(RSUM[:, a % 2, 0:heads], SUM[:, a % 2, 0:heads]).then_inc(s_rs, 1)
                    elif name == "evac":
                        if evac_engine(a) == "dve":
                            evac(dve, i, a)
                    elif name == "tile":
                        key = tile_key(a)
                        if TILE_GROUPS[key][-1] == a:
                            t = GROUPS[a][1]
                            dve.wait_ge(s_pv, i * NG + a + 1)
                            b = bank["out"]
                            if GROUPS[a][0] == "a":
                                dve.tensor_copy(OA[:, tile_tokens(t)], b[:, 0:P]).then_inc(emptied["out"], 1)
                            else:
                                dve.tensor_copy(OB[:, :, tile_tokens(t)], b[:, :].rearrange("p (c q) -> p c q", c=CH)
                                                ).then_inc(emptied["out"], 1)
                    elif name == "wo":
                        b = full(dve, i, ("wo", a))
                        dve.tensor_tensor(XT[1][:, :], XT[2 * a][:, :], b[:, :], ALU.add).then_inc(emptied["single"], 1)
                        taken(dve, i, ("wo", a))
                        shift(XT[1], s_h2)
                    elif name == "mean":
                        b = full(dve, i, ("mean", a))
                        dve.tensor_tensor(HCEN[:, :].rearrange("p (u t) -> p u t", u=PAIR), H[:, :, 0:T],
                                          b[:, :].rearrange("p (u t) -> p u t", u=PAIR), ALU.subtract).then_inc(emptied["single"], 1)
                    elif name == "var":
                        dve.wait_ge(s_hrs, i * DEPTH + a + 1)
                        dve.tensor_tensor(HN[:, :], HCEN[:, :], HRS[:, :], ALU.mult).then_inc(s_hn, 1)
                        dve.wait_ge(s_hn, i * DEPTH + a + 1)
                        dve.tensor_scalar(HG[:, :], HN[:, :], COLS[:, 0, a:a + 1], COLS[:, 1, a:a + 1],
                                          ALU.mult, ALU.add).then_inc(s_hg, 1)
                    elif name == "up":
                        layer, c = a
                        m = HC[c][1]
                        n = layer * len(HC) + c
                        dve.wait_ge(s_gel, i * 6 + n + 1)
                        dve.scalar_tensor_tensor(out=HIDT[0:m, c, :], in0=bank["pair"][0:m, 0:N],
                                                 scalar=B1[0:m, layer, 0, c:c + 1], in1=GEL[0:m, :],
                                                 op0=ALU.add, op1=ALU.mult).then_inc(emptied["pair"], 1)
                    elif name == "down":
                        b = full(dve, i, ("down", a))
                        dve.scalar_tensor_tensor(out=XT[2][:, :], in0=b[:, :], scalar=COLS[:, 2, a:a + 1],
                                                 in1=XT[1][:, :], op0=ALU.add, op1=ALU.add).then_inc(emptied["single"], 1)
                        if a + 1 < DEPTH:
                            taken(dve, i, ("down", a))
                            shift(XT[2], s_x1)
                    elif name == "final":
                        b = full(dve, i, ("final", 0))
                        dve.wait_ge(s_store, 16 * i + 1)
                        dve.tensor_tensor(OUT[:, :, :], b[:, :].rearrange("p (t e) -> p t e", t=TILES),
                                          XR[:, :].rearrange("p (t e) -> p t e", t=TILES), ALU.add).then_inc(emptied["single"], 1)

        @block.tensor
        def _(pe):
            pe.wait_ge(s_weights, 16 * NW[0])
            for w in range(4):
                ins = pe.transpose(bank["turned0"][:, w * P:(w + 1) * P], WA[:, w, :], IDENT)
            ins.then_inc(s_wturn, 1)
            pe.wait_ge(s_wat, 1)
            pe.wait_ge(s_masks, 2)
            pe.wait_ge(s_ones, 8)
            last_b = [[key for key in TILE_GROUPS if key[1] == "b" and key[2] == layer][-1] for layer in range(DEPTH)]
            last_a = [key for key in TILE_GROUPS if key[1] == "a"][-1]
            with pe.Fori(0, turns) as i:
                for name, a in PE_ORDER:
                    if name == "turn_x":
                        for part, (src, ready, per_turn) in enumerate(((XN, s_xn, TILES), (RX, s_rx, 1))):
                            pe.wait_ge(ready, i * per_turn + per_turn)
                            b = take(pe, i, ("turn_x", 0, part))
                            for t in range(TILES):
                                ins = pe.transpose(b[:, tile_tokens(t)], src[:, t, :], IDENT)
                            ins.then_inc(filled[bank_name(("turn_x", 0, part))], 1)
                    elif name == "qkv_a":
                        taken(pe, i, ("turn_x", 0, 1))
                        b = take(pe, i, ("qkv_a", 0))
                        for w in range(2):
                            ins = pe.matmul(b[:, w * N:(w + 1) * N], WAT[:, w, :], RXT[:, :], start=True, stop=True)
                        ins.then_inc(filled["pair"], 1)
                        taken(pe, i, ("turn_x", 0, 0))
                        b = take(pe, i, ("qkv_a_v", 0))
                        for t in range(TILES):
                            ins = pe.matmul(b[:, tile_tokens(t)], XT[0][:, tile_tokens(t)], WAT[:, 2, :], start=True, stop=True)
                        ins.then_inc(filled["single"], 1)
                    elif name == "qkv_b":
                        layer, t = a
                        if layer == 1 and t == 0:
                            pe.wait_ge(s_x1, i + 1)
                        h = H[:, t // 2, (t % 2) * P:(t % 2) * P + P]
                        b = take(pe, i, ("qkv_b", a))
                        for w in range(2):
                            ins = pe.matmul(b[:, w * INNER:(w + 1) * INNER], h, WQKV[:, layer, w * INNER:(w + 1) * INNER],
                                            start=True, stop=True)
                        ins.then_inc(filled["pair"], 1)
                        b = take(pe, i, ("qkv_b_v", a))
                        pe.matmul(b[:, :], h, WQKV[:, layer, 2 * INNER:3 * INNER], start=True, stop=True
                                  ).then_inc(filled["single"], 1)
                    elif name == "turn_qk":
                        layer, t = a
                        pe.wait_ge(s_qkr, i * 8 + layer * TILES + t + 1)
                        for part in range(2):
                            b = take(pe, i, ("turn_qk", a, part))
                            for c in range(CH):
                                n = part * INNER + c * P
                                ins = pe.transpose(b[:, c * P:(c + 1) * P], QKR[:, n:n + P], IDENT)
                            ins.then_inc(filled[bank_name(("turn_qk", a, part))], 1)
                    elif name == "scores":
                        kind, t, p0, heads, keys, k0, layer = GROUPS[a]
                        tok0 = (t // 2) * T + k0
                        if kind == "a":
                            taken(pe, i, ("qkv_a", 0))
                            pe.wait_ge(s_kma, i * HA + HA)
                        else:
                            for part in range(2):
                                taken(pe, i, ("turn_qk", (layer, TILES - 1), part))
                        b = take(pe, i, ("scores", a))
                        pe.matmul(b[:, 0:heads * keys], IDENT_B[:, :], mask(f"mask_{kind}{t % 2}"), start=True, stop=False)
                        if kind == "a":
                            ins = pe.matmul(b[:, 0:heads * keys], QA[:, tile_tokens(t)],
                                            KMA[:, p0:p0 + heads, tok0:tok0 + keys], start=False, stop=True)
                        else:
                            for n in range(heads // 2):
                                ins = pe.matmul(b[:, 2 * n * keys:2 * (n + 1) * keys], QB[:, p0 // 2 + n, tile_tokens(t)],
                                                KMB[:, p0 // 2 + n, :, tok0:tok0 + keys], start=False, stop=n == heads // 2 - 1)
                        ins.then_inc(filled[bank_name(("scores", a))], 1)
                    elif name == "turn_p":
                        kind, t, p0, heads, keys, k0, layer = GROUPS[a]
                        pe.wait_ge(s_prob, i * NG + a + 1)
                        b = take(pe, i, ("turn_p", a))
                        blocks = t % 2 + 1
                        for h in range(heads):
                            for kb in range(blocks):
                                n = h * blocks + kb
                                ins = pe.transpose(b[:, n * P:(n + 1) * P], prob_block(a, h, kb), IDENT)
                        ins.then_inc(filled[bank_name(("turn_p", a))], 1)
                    elif name == "values":
                        kind, t, p0, heads, keys, k0, layer = GROUPS[a]
                        taken(pe, i, ("turn_p", a))
                        key = tile_key(a)
                        if TILE_GROUPS[key][0] == a:
                            if kind == "a":
                                taken(pe, i, ("qkv_a_v", 0))
                            else:
                                taken(pe, i, ("qkv_b_v", (layer, TILES - 1)))
                            take(pe, i, key)
                        b = bank["out"]
                        blocks = t % 2 + 1
                        for h in range(heads):
                            for kb in range(blocks):
                                n = h * blocks + kb
                                pt = PT[a % 2][:, n * P:(n + 1) * P]
                                v_tile = 2 * (t // 2) + kb
                                if kind == "a":
                                    head = causal_position(p0 + h)
                                    j, q = head // 4, head % 4
                                    ins = pe.matmul(b[32 * j:32 * j + 32, 0:P], VA[:, v_tile, 32 * head:32 * head + 32], pt,
                                                    start=q == 0 and kb == 0, stop=q == 3 and kb == blocks - 1,
                                                    tile_position=(0, 32 * j))
                                else:
                                    head = p0 + h
                                    c, s = head // 2, head % 2
                                    ins = pe.matmul(b[64 * s:64 * s + 64, c * P:(c + 1) * P],
                                                    VB[:, v_tile, DB * head:DB * head + DB], pt,
                                                    start=kb == 0, stop=kb == blocks - 1, tile_position=(0, 64 * s))
                        ins.then_inc(s_pv, 1)
                    elif name == "wo":
                        taken(pe, i, last_b[a])
                        b = take(pe, i, ("wo", a))
                        for c in range(CH):
                            ins = pe.matmul(b[:, :], WO[:, a, c, :], OB[:, c, :], start=c == 0, stop=c == CH - 1)
                        ins.then_inc(filled["single"], 1)
                    elif name == "mean":
                        pe.wait_ge(s_h2, i * DEPTH + a + 1)
                        b = take(pe, i, ("mean", a))
                        pe.matmul(b[:, :], MEAN[:, :], H[:, :, 0:T], start=True, stop=True).then_inc(filled["single"], 1)
                    elif name == "var":
                        pe.wait_ge(s_hsq, i * DEPTH + a + 1)
                        b = take(pe, i, ("var", a))
                        pe.matmul(b[:, :], MEAN[:, :], HSQ[:, :], start=True, stop=True).then_inc(filled["single"], 1)
                    elif name == "up":
                        layer, c = a
                        h0, m = HC[c]
                        pe.wait_ge(s_hg, i * DEPTH + layer + 1)
                        b = take(pe, i, ("up", a))
                        for g in range(2):
                            ins = pe.matmul(b[0:m, g * N:(g + 1) * N], W1[:, layer, g * HID + h0:g * HID + h0 + m], HG[:, :],
                                            start=True, stop=True)
                        ins.then_inc(filled["pair"], 1)
                    elif name == "down":
                        taken(pe, i, ("up", (a, len(HC) - 1)))
                        b = take(pe, i, ("down", a))
                        for c, (h0, m) in enumerate(HC):
                            ins = pe.matmul(b[:, :], W2[0:m, a, c, :], HIDT[0:m, c, :], start=c == 0, stop=c == len(HC) - 1)
                        ins.then_inc(filled["single"], 1)
                    elif name == "final":
                        taken(pe, i, last_a)
                        taken(pe, i, ("down", DEPTH - 1))
                        b = take(pe, i, ("final", 0))
                        for t in range(TILES):
                            pe.matmul(b[:, tile_tokens(t)], OA[:, tile_tokens(t)], WAT[:, 3, :], start=True, stop=False)
                            ins = pe.matmul(b[:, tile_tokens(t)], XT[2][:, tile_tokens(t)], IDENT, start=False, stop=True)
                        ins.then_inc(filled["single"], 1)


_INS = ["L0_attn_input", "L0_attn_Wq", "L0_attn_Wk", "L0_attn_Wv", "L0_attn_Wo", "L0_attn_bo", "L0_ffn_wqkv",
        "L0_ffn_q_scale", "L0_ffn_k_scale", "L0_ffn_wo", "L0_ffn_ln_g", "L0_ffn_ln_b", "L0_ffn_w1", "L0_ffn_b1",
        "L0_ffn_w2", "L0_ffn_b2"]


def kernel(**inputs):
    import numpy as _np
    import concourse.bacc as _bacc
    from concourse import mybir as _mybir
    from concourse.bass_utils import run_bass_kernel_spmd as _run

    nc = _bacc.Bacc("TRN2", target_bir_lowering=False, num_devices=1)
    arrays, args = {}, []
    for name in _INS:
        a = _np.ascontiguousarray(inputs[name])
        arrays[f"in_{name}"] = a
        args.append(nc.dram_tensor(f"in_{name}", a.shape, _mybir.dt.from_np(a.dtype), kind="ExternalInput").ap())
    _, c = shape_constants()
    arrays["in_constants"] = c
    args.append(nc.dram_tensor("in_constants", c.shape, _mybir.dt.float32, kind="ExternalInput").ap())
    out = nc.dram_tensor("out_0", inputs["L0_attn_input"].shape, _mybir.dt.float32, kind="ExternalOutput")
    program(nc, *args, out.ap())
    r = _run(nc, [arrays], core_ids=[0])
    return _np.asarray(r.results[0]["out_0"])
```

```python
from contextlib import ExitStack

import numpy as np
import concourse.bass as bass
from concourse import mybir

ALU = mybir.AluOpType
ACT = mybir.ActivationFunctionType
AX_X = mybir.AxisListType.X
F32 = mybir.dt.float32
BF16 = mybir.dt.bfloat16

P = 128
T = 256
PAIR = 2
TILES = PAIR * T // P
N = PAIR * T
HA, DA = 16, 8
HB, DB = 8, 64
WIN = 64
DEPTH = 2
INNER = HB * DB
CH = INNER // P
HID = 341
HC = [(0, 128), (128, 128), (256, 85)]
NEG = -1.0e30
EPS = 1e-5
LN2 = float(np.log(2.0))


def shape_constants():
    f = np.float32
    t = np.arange(T, dtype=f)
    theta = np.repeat(f(10000.0) ** (-np.arange(0, P, 2, dtype=f) / f(P)), 2).astype(f)
    ang = (t[:, None] * theta[None, :]).astype(f)
    cos_a, sin_a = np.cos(ang), np.sin(ang)
    sin_a[:, 0::2] *= -1
    half = np.arange(0, DB, 2, dtype=f)
    inv = (f(1.0) / f(10000.0) ** (half / f(DB))).astype(f)
    fr = (t[:, None] * inv[None, :]).astype(f)
    fr = np.concatenate([fr, fr], -1)
    base = ((half + f(0.4 * DB)) / f(1.4 * DB)).astype(f)
    sc = base[None, :] ** ((t - T // 2) / f(WIN // 2))[:, None].astype(f)
    sc = np.concatenate([sc, sc], -1).astype(f)
    sign = np.ones(DB, f)
    sign[:DB // 2] = -1
    cos_b = np.stack([np.cos(fr) * sc * 8, np.cos(fr) / sc], 1)
    sin_b = np.stack([np.sin(fr) * sign * sc * 8, np.sin(fr) * sign / sc], 1)
    halves = lambda a: a.reshape(2, P, -1).transpose(1, 0, 2).reshape(P, -1)
    row = np.arange(P)
    head = np.stack([(row // DA == h) / np.sqrt(DA) for h in range(HA)], 1)
    q, k = row[:, None], row[None, :]
    causal = np.where(k <= q, 0, NEG)
    first = np.where((k <= q) & (k >= q - WIN), 0, NEG)
    second = np.where((k <= q % WIN + WIN) & (k >= q % WIN), 0, NEG)
    parts = [
        ("ident", np.eye(P)), ("cos_a", halves(cos_a)), ("sin_a", halves(sin_a)), ("head", head),
        ("cos_b", halves(cos_b)), ("sin_b", halves(sin_b)),
        ("mask_a", np.tile(causal, (1, 4))),
        ("mask_b0", np.tile(first, (1, 4))), ("mask_b1", np.tile(second, (1, 4))),
    ]
    at, n = {}, 0
    for name, a in parts:
        at[name] = (n, n + a.shape[1])
        n += a.shape[1]
    return at, np.ascontiguousarray(np.concatenate([a for _, a in parts], 1).astype(f))


FRONT = [("norm", 0), ("rotate", 0), ("turn_x", 0), ("turn_rx", 0), ("qk_a", 0), ("v_a", 0),
         ("mask_k", 0), ("mask_k", 1), ("mask_k", 2), ("mask_k", 3)]
GROUPS = []


def _schedule():
    out = []

    def att(kind, t, g, layer):
        heads, keys = (2, T) if kind == "a" and t % 2 else (4, P)
        GROUPS.append((kind, t, g * heads, heads, keys, layer))
        out.append(("att", len(GROUPS) - 1))

    for layer in range(DEPTH):
        last = layer == DEPTH - 1
        for t in range(TILES):
            out.append(("proj", (layer, t)))
            for g in range(2):
                if t < 2:
                    att("a", 2 * layer, 2 * t + g, layer)
                else:
                    att("b", t - 2, g, layer)
                if g == 0:
                    out.append(("sum_qk", (layer, t)))
                    out.append(("guess_qk", (layer, t)))
                    if t % 2:
                        out.append(("mid_v", (layer, t)))
            if t:
                out.append(("turn_qk", (layer, t - 1)))
            out.append(("rot_qk", (layer, t)))
        att("b", 2, 0, layer)
        att("b", 2, 1, layer)
        out.append(("turn_qk", (layer, TILES - 1)))
        att("b", 3, 0, layer)
        att("b", 3, 1, layer)
        ups = [("up", (layer, c)) for c in range(len(HC))]
        if last:
            tail = [("norm", 0), 2, ("rotate", 0), 2, "wo", 2, "mean", ("turn_rx", 0), 1, "square", ("turn_x", 0), 1, "var",
                    ("qk_a", 0), ("drain", 0), ("v_a", 0), ("mask_k", 0), ("mask_k", 1), ups, ("proj_a", 0), "down",
                    ("mask_k", 2), ("mask_k", 3)]
        else:
            tail = [4, "wo", 1, "mean", 1, "square", "var", 2, ups, "down", ("drain", 1)]
        g = 0
        for item in tail:
            if isinstance(item, int):
                for _ in range(item):
                    att("a", 2 * layer + 1, g, layer)
                    g += 1
            elif isinstance(item, list):
                out += item
            elif isinstance(item, tuple):
                out.append(item)
            else:
                out.append((item, layer))
    return out + [("final", 0), ("residual", 0)]


SCHEDULE = _schedule()
NG = len(GROUPS)
RING = 3
PROLOGUE = FRONT + [("residual", 0)]
LAST = [item for item in SCHEDULE if item not in PROLOGUE]


def with_lags(schedule, **lags):
    out, last, done = [], -1, {name: 0 for name in lags}

    def phases(step):
        for name, lag in lags.items():
            while done[name] <= min(step - lag, last):
                out.append((name, done[name]))
                done[name] += 1

    for item in schedule:
        if item[0] == "att":
            last = item[1]
            phases(last)
        elif item[0] == "drain":
            for step in range(last + 1, last + 1 + (item[1] or max(lags.values(), default=0))):
                phases(step)
        else:
            out.append(item)
    return out


PE_LAGS = dict(scores=0, turn_o=4, turn_p=2, values=3)


def tile_key(k):
    kind, t, _, _, _, layer = GROUPS[k]
    return ("out", kind, layer, t)


def _tile_groups():
    found = {}
    for k in range(NG):
        found.setdefault(tile_key(k), []).append(k)
    return found


TILE_GROUPS = _tile_groups()
OUTPUTS = list(TILE_GROUPS)
NO = len(OUTPUTS)


def last_of_tile(k):
    return TILE_GROUPS[tile_key(k)][-1] == k


def output_number(k):
    return OUTPUTS.index(tile_key(k))


BANKS = ("scores0", "scores1", "turned0", "turned1", "pair", "single", "out")


def bank_turns(schedule):
    turn, count = {}, dict.fromkeys(BANKS, 0)

    def use(bank, key):
        turn[key] = (bank, count[bank])
        count[bank] += 1

    ring = 0
    for name, a in with_lags(schedule, **PE_LAGS):
        if name == "scores":
            use(f"scores{a % 2}", ("scores", a))
        elif name == "values":
            if TILE_GROUPS[tile_key(a)][0] == a:
                use("out", tile_key(a))
        elif name in ("turn_p", "turn_x", "turn_rx", "turn_qk") or name == "turn_o" and last_of_tile(a):
            for part in range(2 if name == "turn_qk" else 1):
                use(f"turned{ring % 2}", (name, a, part))
                ring += 1
        elif name == "qk_a":
            use("pair", (name, a))
        elif name == "proj":
            use("pair", (name, a, 0))
            use("single", (name, a, 1))
        elif name == "up":
            if a[1] == 0:
                use("pair", (name, a))
            else:
                for part in range(2):
                    use(f"scores{part}" if a[1] == 1 else f"turned{(ring + part) % 2}", (name, a, part))
                ring += 2 if a[1] == 2 else 0
        elif name in ("v_a", "mid_v", "wo", "mean", "var", "down", "final"):
            use("single", (name, a))
        elif name == "proj_a":
            use("out", (name, a))
    return turn, count


class Turn:

    def __init__(self, schedule, i, f):
        self.schedule, self.i, self.f = schedule, i, f
        self.use, _ = bank_turns(schedule)
        if schedule is PROLOGUE:
            self.base = dict.fromkeys(BANKS, 0)
        else:
            first, per = bank_turns(PROLOGUE)[1], bank_turns(SCHEDULE)[1]
            self.base = {n: i * per[n] + first[n] for n in BANKS}

    def order(self, key):
        n, k = self.use[key]
        return n, self.base[n] + k

    def bank(self, key):
        return self.use[key][0]


def program(nc, x, wq, wk, wv, wo_a, bo, wqkv, qs, ks, wo, lg, lb, w1, b1, w2, b2, consts, out):
    at, _ = shape_constants()
    turns = x.shape[0] // PAIR
    with ExitStack() as ctx:
        def sb(name, shape, dt=F32):
            return ctx.enter_context(nc.sbuf_tensor(name, shape, dt))

        def sem(name):
            return ctx.enter_context(nc.semaphore(name))

        kept, width = at["head"][1], consts.shape[1]
        CONST = sb("CONST", [P, kept])
        MASKS = sb("MASKS", [P, width - at["mask_a"][0]], BF16)
        IDENT_B = sb("IDENT_B", [P, P], BF16)
        MEAN = sb("MEAN", [P, P])
        WAT = sb("WAT", [P, 4, P])
        WQKV = sb("WQKV", [P, DEPTH, 3 * INNER])
        WO = sb("WO", [P, DEPTH, CH, P])
        W1 = sb("W1", [P, DEPTH, 2 * HID])
        W2 = sb("W2", [P, DEPTH, len(HC), P])
        B1 = sb("B1", [P, DEPTH, 2, len(HC)])
        COLS = sb("COLS", [P, 3, DEPTH])
        BO = sb("BO", [P, P])
        QKS = sb("QKS", [P, DEPTH, 2, DB])
        COS_B = sb("COS_B", [P, DEPTH, 2, 2, DB])
        SIN_B = sb("SIN_B", [P, DEPTH, 2, 2, DB])
        EPS_C = sb("EPS_C", [P, 1])
        LIFT_C = sb("LIFT_C", [P, 1])
        X = sb("X", [P, TILES, P])
        XR = sb("XR", [P, TILES, P])
        XN = sb("XN", [P, TILES, P])
        ROT1 = sb("ROT1", [P, TILES, P])
        ROT2 = sb("ROT2", [P, TILES, P])
        RX = ROT1
        STATS = sb("STATS", [P, TILES, 6])
        WAITED = sb("WAITED", [P, 1])
        MV = sb("MV", [P, TILES, 2])
        NV = sb("NV", [P, 6, TILES])
        XT = [sb(f"XT{n}", [P, N]) for n in range(3)]
        RXT = sb("RXT", [P, N])
        QA = sb("QA", [P, N])
        KA = sb("KA", [P, N])
        KMA = sb("KMA", [P, HA, N])
        VA = sb("VA", [P, TILES, P])
        OA = sb("OA", [P, N])
        H = sb("H", [P, PAIR, T + 1])
        SQ = sb("SQ", [P, 2 * INNER])
        NN = sb("NN", [P, 7, 2 * HB])
        AN = sb("AN", [P, 2, 2 * INNER])
        T1 = sb("T1", [P, 2 * INNER])
        T2 = sb("T2", [P, 2 * INNER])
        QKR = T1
        QB = sb("QB", [P, CH, N])
        KMB = sb("KMB", [P, CH, 2, N])
        VB = sb("VB", [P, PAIR, 3, INNER])
        OB = sb("OB", [P, CH, N])
        PROB = [sb(f"PROB{n}", [P, 512]) for n in range(RING)]
        PT = [sb(f"PT{n}", [P, 512]) for n in range(2)]
        NMAX = sb("NMAX", [P, RING, 4])
        SUM = sb("SUM", [P, RING, HA])
        RSUM = sb("RSUM", [P, HA])
        ON = sb("ON", [P, INNER])
        HLN, HRS = SQ[:, 0:N], SQ[:, N:2 * N]
        HSQ, HNEW = AN[:, 0, 0:N], AN[:, 0, N:2 * N]
        HN, HG = T2[:, 0:N], T2[:, N:2 * N]
        HCEN = sb("HCEN", [P, N])
        GEL = sb("GEL", [P, 2, N])
        HIDT = sb("HIDT", [P, len(HC), N])
        OUT = sb("OUT", [P, TILES, P])

        WA = QB[:, :, 0:P]
        STAGE = KMA[:, :, :].rearrange("p h n -> p (h n)")

        def table(name):
            a, b = at[name]
            return CONST[:, a:b] if b <= kept else STAGE[:, a - kept:b - kept]

        def mask(name):
            return MASKS[:, at[name][0] - at["mask_a"][0]:at[name][1] - at["mask_a"][0]]

        IDENT = table("ident")

        bank = {name: ctx.enter_context(nc.psum_tensor("ps_" + name, [P, 1024 if name == "pair" else 512], F32))
                for name in BANKS}
        filled = {n: sem("filled_" + n) for n in BANKS}
        emptied = {n: sem("emptied_" + n) for n in BANKS}

        x_loaded, weights_loaded, out_stored = sem("x_loaded"), sem("weights_loaded"), sem("out_stored")
        constants_ready, masks_ready, tables_ready = sem("constants_ready"), sem("masks_ready"), sem("tables_ready")
        weights_turned, wat_ready = sem("weights_turned"), sem("wat_ready")
        stats_ready, mv_ready, var_ready = sem("stats_ready"), sem("mv_ready"), sem("var_ready")
        var_ln, rstd_guess, rstd_step, xn_ready = sem("var_ln"), sem("rstd_guess"), sem("rstd_step"), sem("xn_ready")
        rotated_parts, rx_ready, residual_ready = sem("rotated_parts"), sem("rx_ready"), sem("residual_ready")
        attention_projected, attention_added = sem("attention_projected"), sem("attention_added")
        masked_keys_ready = sem("masked_keys_ready")
        squares_ready, norm_sums, norm2_ready, norm_ln = (sem(n) for n in ("squares_ready", "norm_sums", "norm2_ready", "norm_ln"))
        norm_guess, norm_step, unit_ready = sem("norm_guess"), sem("norm_step"), sem("unit_ready")
        cos_part, sin_part, rotated_ready = sem("cos_part"), sem("sin_part"), sem("rotated_ready")
        max_ready, sums_inverted, values_done = sem("max_ready"), sem("sums_inverted"), sem("values_done")
        input_shifted, mid_shifted = sem("input_shifted"), sem("mid_shifted")
        centred_squares, hvar_ln, hrstd_guess, hrstd_square, hnew_scaled, hscaled, hnorm, hg_ready = (sem(n) for n in (
            "centred_squares", "hvar_ln", "hrstd_guess", "hrstd_square", "hnew_scaled", "hscaled", "hnorm", "hg_ready"))
        gelu_ready, hidden_ready = sem("gelu_ready"), sem("hidden_ready")

        block = ctx.enter_context(nc.Block())
        x_view = x.rearrange("(i b) (h p) e -> i p (b h) e", b=PAIR, p=P)
        out_view = out.rearrange("(i b) (h p) e -> i p (b h) e", b=PAIR, p=P)

        def take(e, w, key):
            n, k = w.order(key)
            e.wait_ge(emptied[n], k + 1)
            return bank[n]

        def full(e, w, key):
            n, k = w.order(key)
            e.wait_ge(filled[n], k + 1)
            return bank[n]

        def taken(e, w, key):
            n, k = w.order(key)
            e.wait_ge(emptied[n], k + 2)

        def all_turns(e, work):
            work(Turn(PROLOGUE, 0, 0))
            with e.Fori(0, turns - 1) as i:
                work(Turn(SCHEDULE, i, i + 1))
            work(Turn(LAST, turns - 1, turns))

        def tokens(t):
            return slice(t * P, (t + 1) * P)

        def by_tile(a):
            return a.rearrange("p (t e) -> p t e", e=P)

        def evac_by_act(k):
            return k % 2 == 0

        def up_banks(w, key):
            if key[1] == 0:
                return bank["pair"][:, 0:N], bank["pair"][:, N:2 * N]
            return [bank[w.bank(("up", key, part))] for part in range(2)]

        @block.sync
        def _(sp):
            sp.dma_start(CONST[:, :], consts[:, 0:kept]).then_inc(weights_loaded, 16)
            sp.dma_start(STAGE[:, 0:width - kept], consts[:, kept:width]).then_inc(weights_loaded, 16)
            for n, w in enumerate((wq, wk, wv, wo_a)):
                sp.dma_start(WA[:, n, :], w).then_inc(weights_loaded, 16)
            sp.dma_start(X[:, :, :], x_view[0]).then_inc(x_loaded, 16)
            sp.dma_start(BO[:, :], bo.rearrange("(a n) -> a n", a=1).to_broadcast([P, P])).then_inc(weights_loaded, 16)
            for layer in range(DEPTH):
                for n, v in enumerate((qs, ks)):
                    sp.dma_start(QKS[:, layer, n, :], v[layer:layer + 1, :].to_broadcast([P, DB])).then_inc(weights_loaded, 16)
                sp.dma_start(WQKV[:, layer, :], wqkv[layer]).then_inc(weights_loaded, 16)
                sp.dma_start(WO[:, layer, :, :], wo[layer].rearrange("(c p) n -> p c n", p=P)).then_inc(weights_loaded, 16)
                sp.dma_start(W1[:, layer, :], w1[layer]).then_inc(weights_loaded, 16)
                for c, (a, m) in enumerate(HC):
                    sp.dma_start(W2[0:m, layer, c, :], w2[layer, a:a + m, :]).then_inc(weights_loaded, 16)
                    for g in range(2):
                        sp.dma_start(B1[0:m, layer, g, c:c + 1], b1[layer, g * HID + a:g * HID + a + m].rearrange(
                            "(p a) -> p a", a=1)).then_inc(weights_loaded, 16)
                for n, v in enumerate((lg, lb, b2)):
                    sp.dma_start(COLS[:, n, layer:layer + 1], v[layer].rearrange("(p a) -> p a", a=1)).then_inc(weights_loaded, 16)
            with sp.Fori(1, turns) as f:
                sp.wait_ge(xn_ready, f * TILES)
                sp.wait_ge(residual_ready, f)
                sp.dma_start(X[:, :, :], x_view[f]).then_inc(x_loaded, 16)

        ALL_WEIGHTS = 16 * (7 + DEPTH * (5 + 3 * len(HC) + 3))

        @block.gpsimd
        def _(pool):
            for n in BANKS:
                pool.sem_inc(emptied[n], 1)
            pool.sem_inc(out_stored, 1)
            pool.memset(MEAN[:, :], 1.0 / P).then_inc(constants_ready, 1)
            pool.memset(EPS_C[:, :], EPS).then_inc(constants_ready, 1)
            pool.memset(LIFT_C[:, :], 10 * LN2).then_inc(constants_ready, 1)
            pool.memset(H[:, :, :], 0.0).then_inc(constants_ready, 1)
            pool.memset(KMB[:, :, :, :], 0.0).then_inc(constants_ready, 1)
            pool.wait_ge(weights_loaded, ALL_WEIGHTS)

            def work(w):
                i, f = w.i, w.f
                for name, a in w.schedule:
                    if name == "rotate":
                        pool.wait_ge(xn_ready, f * TILES + TILES)
                        for u in range(PAIR):
                            two = slice(2 * u, 2 * u + 2)
                            cos, sin = by_tile(table("cos_a")), by_tile(table("sin_a"))
                            pool.tensor_tensor(ROT1[:, two, :], XN[:, two, :], cos, ALU.mult).then_inc(rotated_parts, 1)
                            for odd in range(2):
                                pool.tensor_tensor(ROT2[:, two, odd::2], XN[:, two, 1 - odd::2], sin[:, :, odd::2],
                                                   ALU.mult).then_inc(rotated_parts, 1)
                        pool.wait_ge(rotated_parts, f * 6 + 6)
                        pool.tensor_tensor(RX[:, :, :], ROT1[:, :, :], ROT2[:, :, :], ALU.add).then_inc(rx_ready, 1)
                    elif name == "residual":
                        if w.schedule is not PROLOGUE:
                            taken(pool, w, ("final", 0))
                        else:
                            pool.wait_ge(x_loaded, 16)
                        pool.tensor_tensor(XR[:, :, :], X[:, :, :], BO[:, None, :].to_broadcast([P, TILES, P]),
                                           ALU.add).then_inc(residual_ready, 1)
                    elif name == "rot_qk":
                        layer, t = a
                        n = layer * TILES + t
                        if n:
                            full(pool, w, ("turn_qk", ((n - 1) // TILES, (n - 1) % TILES), 0))
                        pool.wait_ge(unit_ready, i * 8 + n + 1)
                        pool.tensor_tensor(T1[:, :].rearrange("p (s h d) -> p s h d", s=2, d=DB),
                                           AN[:, t % 2, :].rearrange("p (s h d) -> p s h d", s=2, d=DB),
                                           COS_B[:, layer, t % 2, :, None, :].to_broadcast([P, 2, HB, DB]),
                                           ALU.mult).then_inc(cos_part, 1)
                        pool.wait_ge(cos_part, i * 8 + n + 1)
                        pool.wait_ge(sin_part, i * 16 + 2 * n + 2)
                        pool.tensor_tensor(QKR[:, :], T1[:, :], T2[:, :], ALU.add).then_inc(rotated_ready, 1)

            all_turns(pool, work)

        @block.scalar
        def _(act):
            act.wait_ge(weights_loaded, ALL_WEIGHTS)
            act.wait_ge(constants_ready, 5)
            act.preload_act_table_set("natural_log_exp_and_others")

            def work(w):
                i, f = w.i, w.f
                for name, a in with_lags(w.schedule, evac_o=4, evac=2, exponentials=0):
                    if name == "norm":
                        act.wait_ge(var_ready, f + 1)
                        act.activation(NV[:, 1, :], NV[:, 0, :], ACT.Ln).then_inc(var_ln, 1)
                        act.wait_ge(var_ln, f + 1)
                        act.activation(NV[:, 2, :], NV[:, 1, :], ACT.Exp, scale=-0.5).then_inc(rstd_guess, 1)
                    elif name == "turn_x":
                        b = full(act, w, ("turn_x", 0, 0))
                        act.activation(XT[0][:, :], b[:, :], ACT.Copy)
                        bt = b[:, :].rearrange("p (u t) -> p u t", u=PAIR)
                        act.activation(H[0:64, :, 0:T], bt[0:64], ACT.Copy)
                        act.activation(H[64:P, :, 1:T + 1], bt[64:P], ACT.Copy).then_inc(emptied[w.bank(("turn_x", 0, 0))], 1)
                    elif name == "turn_rx":
                        b = full(act, w, ("turn_rx", 0, 0))
                        act.activation(RXT[:, :], b[:, :], ACT.Copy).then_inc(emptied[w.bank(("turn_rx", 0, 0))], 1)
                    elif name == "qk_a":
                        b = full(act, w, ("qk_a", 0))
                        act.activation(QA[:, :], b[:, 0:N], ACT.Copy)
                        act.activation(KA[:, :], b[:, N:2 * N], ACT.Copy).then_inc(emptied["pair"], 1)
                    elif name == "proj":
                        layer, t = a
                        n = layer * TILES + t
                        b = full(act, w, ("proj", a, 0))
                        act.activation(SQ[:, :], b[:, :], ACT.Square).then_inc(squares_ready, 1)
                        if n >= 2:
                            act.wait_ge(cos_part, i * 8 + n - 1)
                            act.wait_ge(sin_part, i * 16 + 2 * n - 2)
                        act.activation(AN[:, t % 2, :], b[:, :], ACT.Copy).then_inc(emptied["pair"], 1)
                        b = full(act, w, ("proj", a, 1))
                        act.activation(VB[:, t // 2, 2 * (t % 2), :], b[:, :], ACT.Copy).then_inc(emptied["single"], 1)
                    elif name == "mid_v":
                        b = full(act, w, ("mid_v", a))
                        act.activation(VB[:, a[1] // 2, 1, :], b[:, :], ACT.Copy).then_inc(emptied["single"], 1)
                    elif name == "guess_qk":
                        n = a[0] * TILES + a[1]
                        act.wait_ge(norm2_ready, i * 8 + n + 1)
                        act.activation(NN[:, 2, :], NN[:, 1, :], ACT.Ln, scale=float(2 ** 20)).then_inc(norm_ln, 1)
                        act.wait_ge(norm_ln, i * 8 + n + 1)
                        act.activation(NN[:, 3, :], NN[:, 2, :], ACT.Exp, bias=LIFT_C[:, 0:1], scale=-0.5).then_inc(norm_guess, 1)
                    elif name == "turn_qk":
                        b = full(act, w, ("turn_qk", a, 0))
                        act.activation(QB[:, :, tokens(a[1])], by_tile(b[:, :]), ACT.Copy).then_inc(
                            emptied[w.bank(("turn_qk", a, 0))], 1)
                    elif name == "exponentials":
                        kind, t, h0, heads, keys, layer = GROUPS[a]
                        act.wait_ge(max_ready, i * NG + a + 1)
                        if a >= RING:
                            full(act, w, ("turn_p", a - RING, 0))
                        n = output_number(a)
                        if n >= RING:
                            act.wait_ge(sums_inverted, i * NO + n - RING + 1)
                        b = bank[f"scores{a % 2}"]
                        for h in range(heads):
                            k = slice(h * keys, (h + 1) * keys)
                            ins = act.activation(PROB[a % RING][:, k], b[:, k], ACT.Exp, bias=NMAX[:, a % RING, h:h + 1],
                                                 accum_out=SUM[:, n % RING, h0 + h:h0 + h + 1])
                        ins.then_inc(emptied[f"scores{a % 2}"], 1)
                    elif name == "evac":
                        if evac_by_act(a):
                            b = full(act, w, ("turn_p", a, 0))
                            if a >= 2:
                                act.wait_ge(values_done, i * NG + a - 1)
                            act.activation(PT[a % 2][:, :], b[:, :], ACT.Copy).then_inc(emptied[w.bank(("turn_p", a, 0))], 1)
                    elif name == "evac_o":
                        if last_of_tile(a):
                            t = GROUPS[a][1]
                            key = ("turn_o", a, 0)
                            b = full(act, w, key)
                            if GROUPS[a][0] == "a":
                                act.activation(OA[:, tokens(t)], b[:, 0:P], ACT.Copy).then_inc(emptied[w.bank(key)], 1)
                            else:
                                act.activation(OB[:, :, tokens(t)], by_tile(b[:, :]), ACT.Copy).then_inc(
                                    emptied[w.bank(key)], 1)
                    elif name == "square":
                        taken(act, w, ("mean", a))
                        act.activation(HSQ, HCEN[:, :], ACT.Square).then_inc(centred_squares, 1)
                    elif name == "var":
                        b = full(act, w, ("var", a))
                        act.activation(HLN, b[:, :], ACT.Ln, bias=EPS_C[:, 0:1]).then_inc(hvar_ln, 1)
                        act.wait_ge(hvar_ln, i * DEPTH + a + 1)
                        act.activation(HRS, HLN, ACT.Exp, scale=-0.5).then_inc(hrstd_guess, 1)
                        act.wait_ge(hrstd_guess, i * DEPTH + a + 1)
                        act.activation(HLN, HRS, ACT.Square).then_inc(hrstd_square, 1)
                        taken(act, w, ("var", a))
                        act.activation(HSQ, HNEW, ACT.Copy, bias=1.5, scale=-0.5).then_inc(hnew_scaled, 1)
                    elif name == "up":
                        layer, c = a
                        m = HC[c][1]
                        full(act, w, ("up", a, 1) if c else ("up", a))
                        if c >= 2:
                            act.wait_ge(hidden_ready, i * 6 + layer * len(HC) + c - 1)
                        ins = act.activation(GEL[0:m, c % 2, :], up_banks(w, a)[1][0:m, :], ACT.Gelu,
                                             bias=B1[0:m, layer, 1, c:c + 1])
                        ins.then_inc(gelu_ready, 1)
                        if c == len(HC) - 1:
                            act.preload_act_table_set("natural_log_exp_and_others")
                    elif name == "final":
                        taken(act, w, ("final", 0))
                        act.dma_start(out_view[i], OUT[:, :, :]).then_inc(out_stored, 16)

            all_turns(act, work)
            act.wait_ge(out_stored, 16 * turns + 1)

        @block.vector
        def _(dve):
            def shift(src, done):
                v = src[:, :].rearrange("p (u t) -> p u t", u=PAIR)
                dve.tensor_copy(H[0:64, :, 0:T], v[0:64])
                dve.tensor_copy(H[64:P, :, 1:T + 1], v[64:P]).then_inc(done, 1)

            dve.wait_ge(weights_loaded, ALL_WEIGHTS)
            dve.wait_ge(constants_ready, 5)
            a0 = at["mask_a"][0] - kept
            dve.tensor_copy(MASKS[:, :], STAGE[:, a0:width - kept]).then_inc(masks_ready, 1)
            dve.tensor_copy(IDENT_B[:, :], IDENT).then_inc(masks_ready, 1)
            dve.wait_ge(weights_turned, 1)
            dve.tensor_copy(WAT[:, :, :], by_tile(bank["turned0"][:, :])).then_inc(wat_ready, 1)
            for layer in range(DEPTH):
                for hf in range(2):
                    cos, sin = (table(n).rearrange("p (h s d) -> p h s d", h=2, s=2)[:, hf] for n in ("cos_b", "sin_b"))
                    dve.tensor_tensor(COS_B[:, layer, hf], cos, QKS[:, layer], ALU.mult).then_inc(tables_ready, 1)
                    for o in range(2):
                        d, s = slice(32 * o, 32 * o + 32), slice(32 - 32 * o, 64 - 32 * o)
                        dve.tensor_tensor(SIN_B[:, layer, hf, :, d], sin[:, :, d], QKS[:, layer, :, s],
                                          ALU.mult).then_inc(tables_ready, 1)
            dve.wait_ge(tables_ready, 6 * DEPTH)

            def newton(v, step, before):
                dve.tensor_tensor(v[:, 3, :], v[:, 2, :], v[:, 2, :], ALU.mult).then_inc(step, 1)
                dve.wait_ge(step, before + 1)
                dve.scalar_tensor_tensor(out=v[:, 4, :], in0=v[:, 3, :], scalar=-0.5, in1=v[:, 0, :],
                                         op0=ALU.mult, op1=ALU.mult).then_inc(step, 1)
                dve.wait_ge(step, before + 2)
                dve.scalar_tensor_tensor(out=v[:, 5, :], in0=v[:, 4, :], scalar=1.5, in1=v[:, 2, :],
                                         op0=ALU.add, op1=ALU.mult).then_inc(step, 1)
                dve.wait_ge(step, before + 3)

            def work(w):
                i, f = w.i, w.f
                for name, a in with_lags(w.schedule, maxima=0, evac=2, output=3):
                    if name == "norm":
                        dve.wait_ge(x_loaded, 16 * f + 16)
                        for t in range(TILES):
                            dve.bn_stats(STATS[:, t, :], X[:, t, :]).then_inc(stats_ready, 1)
                        dve.wait_ge(stats_ready, f * TILES + TILES)
                        dve.memset(WAITED[:, :], 0.0)
                        for t in range(TILES):
                            dve.bn_aggr(MV[:, t, :], STATS[:, t, :]).then_inc(mv_ready, 1)
                        dve.wait_ge(mv_ready, f * TILES + TILES)
                        dve.tensor_scalar(NV[:, 0, :], MV[:, :, 1], EPS, None, ALU.add).then_inc(var_ready, 1)
                    elif name == "rotate":
                        dve.wait_ge(rstd_guess, f + 1)
                        newton(NV, rstd_step, f * 3)
                        for t in range(TILES):
                            dve.tensor_scalar(XN[:, t, :], X[:, t, :], MV[:, t, 0:1], NV[:, 5, t:t + 1],
                                              ALU.subtract, ALU.mult).then_inc(xn_ready, 1)
                    elif name == "v_a":
                        b = full(dve, w, ("v_a", 0))
                        dve.tensor_copy(VA[:, :, :], by_tile(b[:, :])).then_inc(emptied["single"], 1)
                    elif name == "mask_k":
                        if a == 0:
                            taken(dve, w, ("qk_a", 0))
                        for p in range(4 * a, 4 * a + 4):
                            dve.tensor_scalar(KMA[:, p, :], KA[:, :], table("head")[:, p:p + 1], None,
                                              ALU.mult).then_inc(masked_keys_ready, 1)
                    elif name == "sum_qk":
                        layer, t = a
                        n = layer * TILES + t
                        dve.wait_ge(squares_ready, i * 8 + n + 1)
                        dve.tensor_reduce(NN[:, 1, :], SQ[:, :].rearrange("p (h d) -> p h d", d=DB), AX_X,
                                          ALU.add).then_inc(norm_sums, 1)
                        dve.wait_ge(norm_sums, i * 8 + n + 1)
                        dve.tensor_scalar(NN[:, 1, :], NN[:, 1, :], 1e-24, None, ALU.max).then_inc(norm2_ready, 1)
                    elif name == "rot_qk":
                        layer, t = a
                        n = layer * TILES + t
                        dve.wait_ge(norm_guess, i * 8 + n + 1)
                        newton(NN[:, 1:7, :], norm_step, (i * 8 + n) * 3)
                        taken(dve, w, ("proj", a, 0))
                        an = AN[:, t % 2, :].rearrange("p (h d) -> p h d", d=DB)
                        dve.tensor_tensor(an, an, NN[:, 6, :, None].to_broadcast([P, 2 * HB, DB]),
                                          ALU.mult).then_inc(unit_ready, 1)
                        dve.wait_ge(unit_ready, i * 8 + n + 1)
                        if n:
                            dve.wait_ge(rotated_ready, i * 8 + n)
                        an = AN[:, t % 2, :].rearrange("p (s h d) -> p s h d", s=2, d=DB)
                        t2 = T2[:, :].rearrange("p (s h d) -> p s h d", s=2, d=DB)
                        for o in range(2):
                            d, s = slice(32 * o, 32 * o + 32), slice(32 - 32 * o, 64 - 32 * o)
                            dve.tensor_tensor(t2[:, :, :, d], an[:, :, :, s],
                                              SIN_B[:, layer, t % 2, :, None, d].to_broadcast([P, 2, HB, 32]),
                                              ALU.mult).then_inc(sin_part, 1)
                    elif name == "turn_qk":
                        layer, t = a
                        b = by_tile(full(dve, w, ("turn_qk", a, 1))[:, :])
                        dve.tensor_copy(KMB[0:64, :, 0, tokens(t)], b[0:64])
                        dve.tensor_copy(KMB[64:P, :, 1, tokens(t)], b[64:P]).then_inc(emptied[w.bank(("turn_qk", a, 1))], 1)
                    elif name == "maxima":
                        kind, t, h0, heads, keys, layer = GROUPS[a]
                        b = full(dve, w, ("scores", a))
                        if a >= RING:
                            taken(dve, w, ("scores", a - RING))
                        dve.tensor_reduce(NMAX[:, a % RING, 0:heads],
                                          b[:, :].rearrange("p (h k) -> p h k", h=heads), AX_X,
                                          ALU.max, negate=True).then_inc(max_ready, 1)
                    elif name == "evac":
                        if not evac_by_act(a):
                            b = full(dve, w, ("turn_p", a, 0))
                            if a >= 2:
                                dve.wait_ge(values_done, i * NG + a - 1)
                            dve.tensor_copy(PT[a % 2][:, :], b[:, :]).then_inc(emptied[w.bank(("turn_p", a, 0))], 1)
                    elif name == "output":
                        if last_of_tile(a):
                            n = output_number(a)
                            heads, d = (HA, DA) if GROUPS[a][0] == "a" else (HB, DB)
                            if n:
                                full(dve, w, ("turn_o", TILE_GROUPS[OUTPUTS[n - 1]][-1], 0))
                            taken(dve, w, ("scores", a))
                            dve.reciprocal(RSUM[:, 0:heads], SUM[:, n % RING, 0:heads]).then_inc(sums_inverted, 1)
                            dve.wait_ge(sums_inverted, i * NO + n + 1)
                            dve.wait_ge(values_done, i * NG + a + 1)
                            dve.tensor_tensor(ON[:, 0:heads * d].rearrange("p (h d) -> p h d", d=d),
                                              bank["out"][:, 0:heads * d].rearrange("p (h d) -> p h d", d=d),
                                              RSUM[:, 0:heads, None].to_broadcast([P, heads, d]),
                                              ALU.mult).then_inc(emptied["out"], 1)
                    elif name == "wo":
                        b = full(dve, w, ("wo", a))
                        dve.tensor_tensor(XT[1][:, :], XT[2 * a][:, :], b[:, :], ALU.add).then_inc(emptied["single"], 1)
                        taken(dve, w, ("wo", a))
                        shift(XT[1], mid_shifted)
                    elif name == "mean":
                        b = full(dve, w, ("mean", a))
                        dve.tensor_tensor(HCEN[:, :].rearrange("p (u t) -> p u t", u=PAIR), H[:, :, 0:T],
                                          b[:, :].rearrange("p (u t) -> p u t", u=PAIR), ALU.subtract).then_inc(emptied["single"], 1)
                    elif name == "var":
                        dve.wait_ge(hrstd_square, i * DEPTH + a + 1)
                        dve.scalar_tensor_tensor(out=HNEW, in0=bank["single"][:, :], scalar=EPS, in1=HLN,
                                                 op0=ALU.add, op1=ALU.mult).then_inc(emptied["single"], 1)
                        dve.tensor_tensor(HN, HCEN[:, :], HRS, ALU.mult).then_inc(hscaled, 1)
                        dve.wait_ge(hscaled, i * DEPTH + a + 1)
                        dve.wait_ge(hnew_scaled, i * DEPTH + a + 1)
                        dve.tensor_tensor(HN, HN, HSQ, ALU.mult).then_inc(hnorm, 1)
                        dve.wait_ge(hnorm, i * DEPTH + a + 1)
                        dve.tensor_scalar(HG, HN, COLS[:, 0, a:a + 1], COLS[:, 1, a:a + 1],
                                          ALU.mult, ALU.add).then_inc(hg_ready, 1)
                    elif name == "up":
                        layer, c = a
                        m = HC[c][1]
                        full(dve, w, ("up", a, 0) if c else ("up", a))
                        dve.wait_ge(gelu_ready, i * 6 + layer * len(HC) + c + 1)
                        dve.scalar_tensor_tensor(out=HIDT[0:m, c, :], in0=up_banks(w, a)[0][0:m, :],
                                                 scalar=B1[0:m, layer, 0, c:c + 1], in1=GEL[0:m, c % 2, :],
                                                 op0=ALU.add, op1=ALU.mult).then_inc(hidden_ready, 1)
                        dve.wait_ge(hidden_ready, i * 6 + layer * len(HC) + c + 1)
                        for key in [("up", a, 0), ("up", a, 1)] if c else [("up", a)]:
                            dve.sem_inc(emptied[w.bank(key)], 1)
                    elif name == "down":
                        b = full(dve, w, ("down", a))
                        dve.scalar_tensor_tensor(out=XT[2][:, :], in0=b[:, :], scalar=COLS[:, 2, a:a + 1],
                                                 in1=XT[1][:, :], op0=ALU.add, op1=ALU.add).then_inc(emptied["single"], 1)
                        if a + 1 < DEPTH:
                            taken(dve, w, ("down", a))
                            shift(XT[2], input_shifted)
                    elif name == "proj_a":
                        b = bank["out"]
                        dve.wait_ge(attention_projected, i + 1)
                        dve.wait_ge(residual_ready, i + 1)
                        dve.tensor_tensor(XR[:, :, :], by_tile(b[:, :]), XR[:, :, :], ALU.add).then_inc(attention_added, 1)
                        dve.wait_ge(attention_added, i + 1)
                        dve.sem_inc(emptied["out"], 1)
                    elif name == "final":
                        b = full(dve, w, ("final", 0))
                        dve.wait_ge(out_stored, 16 * i + 1)
                        dve.wait_ge(attention_added, i + 1)
                        dve.tensor_tensor(OUT[:, :, :], by_tile(b[:, :]), XR[:, :, :], ALU.add).then_inc(emptied["single"], 1)

            all_turns(dve, work)

        @block.tensor
        def _(pe):
            pe.wait_ge(weights_loaded, ALL_WEIGHTS)
            for n in range(4):
                ins = pe.transpose(bank["turned0"][:, n * P:(n + 1) * P], WA[:, n, :], IDENT)
            ins.then_inc(weights_turned, 1)
            pe.wait_ge(wat_ready, 1)
            pe.wait_ge(masks_ready, 2)
            pe.wait_ge(constants_ready, 5)
            last_output = {(key[1], key[2]): ("turn_o", ks[-1], 0) for key, ks in TILE_GROUPS.items()}

            def turn_tiles(w, key, src):
                b = take(pe, w, key)
                for t in range(TILES):
                    ins = pe.transpose(b[:, tokens(t)], src[:, t, :], IDENT)
                ins.then_inc(filled[w.bank(key)], 1)

            def work(w):
                i, f = w.i, w.f
                for name, a in with_lags(w.schedule, **PE_LAGS):
                    if name == "turn_x":
                        pe.wait_ge(xn_ready, f * TILES + TILES)
                        turn_tiles(w, ("turn_x", 0, 0), XN)
                    elif name == "turn_rx":
                        pe.wait_ge(rx_ready, f + 1)
                        turn_tiles(w, ("turn_rx", 0, 0), RX)
                    elif name == "qk_a":
                        taken(pe, w, ("turn_rx", 0, 0))
                        b = take(pe, w, ("qk_a", 0))
                        for n in range(2):
                            ins = pe.matmul(b[:, n * N:(n + 1) * N], WAT[:, n, :], RXT[:, :], start=True, stop=True)
                        ins.then_inc(filled["pair"], 1)
                    elif name == "v_a":
                        taken(pe, w, ("turn_x", 0, 0))
                        b = take(pe, w, ("v_a", 0))
                        for t in range(TILES):
                            ins = pe.matmul(b[:, tokens(t)], XT[0][:, tokens(t)], WAT[:, 2, :], start=True, stop=True)
                        ins.then_inc(filled["single"], 1)
                    elif name == "proj":
                        layer, t = a
                        if layer == 1 and t == 0:
                            pe.wait_ge(input_shifted, i + 1)
                        h = H[:, t // 2, (t % 2) * P:(t % 2) * P + P]
                        b = take(pe, w, ("proj", a, 0))
                        for n in range(2):
                            ins = pe.matmul(b[:, n * INNER:(n + 1) * INNER], h, WQKV[:, layer, n * INNER:(n + 1) * INNER],
                                            start=True, stop=True)
                        ins.then_inc(filled["pair"], 1)
                        b = take(pe, w, ("proj", a, 1))
                        pe.matmul(b[:, :], h, WQKV[:, layer, 2 * INNER:3 * INNER], start=True, stop=True
                                  ).then_inc(filled["single"], 1)
                    elif name == "mid_v":
                        layer, t = a
                        b = take(pe, w, ("mid_v", a))
                        pe.matmul(b[:, :], H[:, t // 2, WIN:WIN + P], WQKV[:, layer, 2 * INNER:3 * INNER],
                                  start=True, stop=True).then_inc(filled["single"], 1)
                    elif name == "turn_qk":
                        layer, t = a
                        pe.wait_ge(rotated_ready, i * 8 + layer * TILES + t + 1)
                        for part in (1, 0):
                            b = take(pe, w, ("turn_qk", a, part))
                            for c in range(CH):
                                n = part * INNER + c * P
                                ins = pe.transpose(b[:, c * P:(c + 1) * P], QKR[:, n:n + P], IDENT)
                            ins.then_inc(filled[w.bank(("turn_qk", a, part))], 1)
                    elif name == "scores":
                        kind, t, h0, heads, keys, layer = GROUPS[a]
                        if kind == "a":
                            if t == 0:
                                pe.wait_ge(masked_keys_ready, i * HA + h0 + heads)
                        else:
                            for part in range(2):
                                taken(pe, w, ("turn_qk", (layer, t), part))
                        b = take(pe, w, ("scores", a))
                        first = t // 2 * T
                        if kind == "a":
                            pe.matmul(b[:, :], QA[:, tokens(t)], KMA[:, h0:h0 + heads, first:first + keys],
                                      start=True, stop=False)
                            own = b[:, :].rearrange("p (h k) -> p h k", h=heads)[:, :, keys - P:keys]
                            ins = pe.matmul(own, IDENT_B[:, :], mask("mask_a")[:, 0:heads * P], start=False, stop=True)
                        else:
                            pe.matmul(b[:, :], IDENT_B[:, :], mask(f"mask_b{t % 2}"), start=True, stop=False)
                        for n in range(heads // 2 if kind == "b" else 0):
                            two, c = slice(2 * n * P, 2 * (n + 1) * P), h0 // 2 + n
                            if t % 2 == 0:
                                ins = pe.matmul(b[:, two], QB[:, c, tokens(t)], KMB[:, c, :, tokens(t)],
                                                start=False, stop=n == 1)
                            else:
                                for s in range(2):
                                    q0, k0 = first + P + s * WIN, first + (1 + s) * WIN
                                    ins = pe.matmul(b[WIN * s:WIN * (s + 1), two], QB[:, c, q0:q0 + WIN],
                                                    KMB[:, c, :, k0:k0 + P], start=False, stop=n == 1,
                                                    tile_position=(0, WIN * s))
                        ins.then_inc(filled[w.bank(("scores", a))], 1)
                    elif name == "turn_p":
                        taken(pe, w, ("scores", a))
                        b = take(pe, w, ("turn_p", a, 0))
                        for n in range(4):
                            ins = pe.transpose(b[:, n * P:(n + 1) * P], PROB[a % RING][:, n * P:(n + 1) * P], IDENT)
                        ins.then_inc(filled[w.bank(("turn_p", a, 0))], 1)
                    elif name == "values":
                        kind, t, h0, heads, keys, layer = GROUPS[a]
                        taken(pe, w, ("turn_p", a, 0))
                        if TILE_GROUPS[tile_key(a)][0] == a:
                            if kind == "b":
                                taken(pe, w, ("mid_v", (layer, t | 1)))
                            take(pe, w, tile_key(a))
                        b = bank["out"]
                        for n in range(4):
                            pt = PT[a % 2][:, n * P:(n + 1) * P]
                            if kind == "a":
                                blocks = keys // P
                                head, kb = h0 + n // blocks, n % blocks
                                ins = pe.matmul(b[:, DA * head:DA * (head + 1)], pt,
                                                VA[:, t // 2 * 2 + kb, DA * head:DA * (head + 1)],
                                                start=kb == 0, stop=kb == blocks - 1)
                            else:
                                d = slice(DB * (h0 + n), DB * (h0 + n + 1))
                                if t % 2 == 0:
                                    ins = pe.matmul(b[:, d], pt, VB[:, t // 2, 0, d], start=True, stop=True)
                                else:
                                    for s in range(2):
                                        q = slice(WIN * s, WIN * (s + 1))
                                        ins = pe.matmul(b[q, d], pt[:, q], VB[:, t // 2, 1 + s, d],
                                                        start=True, stop=True, tile_position=(0, WIN * s))
                        ins.then_inc(values_done, 1)
                    elif name == "turn_o":
                        if last_of_tile(a):
                            taken(pe, w, tile_key(a))
                            key = ("turn_o", a, 0)
                            b = take(pe, w, key)
                            for c in range(1 if GROUPS[a][0] == "a" else CH):
                                ins = pe.transpose(b[:, c * P:(c + 1) * P], ON[:, c * P:(c + 1) * P], IDENT)
                            ins.then_inc(filled[w.bank(key)], 1)
                    elif name == "wo":
                        taken(pe, w, last_output[("b", a)])
                        b = take(pe, w, ("wo", a))
                        for c in range(CH):
                            ins = pe.matmul(b[:, :], WO[:, a, c, :], OB[:, c, :], start=c == 0, stop=c == CH - 1)
                        ins.then_inc(filled["single"], 1)
                    elif name == "mean":
                        pe.wait_ge(mid_shifted, i * DEPTH + a + 1)
                        b = take(pe, w, ("mean", a))
                        pe.matmul(b[:, :], MEAN[:, :], H[:, :, 0:T], start=True, stop=True).then_inc(filled["single"], 1)
                    elif name == "var":
                        pe.wait_ge(centred_squares, i * DEPTH + a + 1)
                        b = take(pe, w, ("var", a))
                        pe.matmul(b[:, :], MEAN[:, :], HSQ, start=True, stop=True).then_inc(filled["single"], 1)
                    elif name == "up":
                        layer, c = a
                        h0, m = HC[c]
                        pe.wait_ge(hg_ready, i * DEPTH + layer + 1)
                        if c:
                            for part in range(2):
                                take(pe, w, ("up", a, part))
                        else:
                            take(pe, w, ("up", a))
                        for g in (1, 0):
                            ins = pe.matmul(up_banks(w, a)[g][0:m, :], W1[:, layer, g * HID + h0:g * HID + h0 + m], HG,
                                            start=True, stop=True)
                            if c:
                                ins.then_inc(filled[w.bank(("up", a, g))], 1)
                        if c == 0:
                            ins.then_inc(filled["pair"], 1)
                    elif name == "down":
                        b = take(pe, w, ("down", a))
                        for c, (h0, m) in enumerate(HC):
                            pe.wait_ge(hidden_ready, i * 6 + a * len(HC) + c + 1)
                            ins = pe.matmul(b[:, :], W2[0:m, a, c, :], HIDT[0:m, c, :], start=c == 0, stop=c == len(HC) - 1)
                        ins.then_inc(filled["single"], 1)
                    elif name == "proj_a":
                        taken(pe, w, last_output[("a", DEPTH - 1)])
                        b = take(pe, w, ("proj_a", 0))
                        for t in range(TILES):
                            ins = pe.matmul(b[:, tokens(t)], OA[:, tokens(t)], WAT[:, 3, :], start=True, stop=True)
                        ins.then_inc(attention_projected, 1)
                    elif name == "final":
                        taken(pe, w, ("down", DEPTH - 1))
                        b = take(pe, w, ("final", 0))
                        for t in range(TILES):
                            ins = pe.transpose(b[:, tokens(t)], XT[2][:, tokens(t)], IDENT)
                        ins.then_inc(filled["single"], 1)

            all_turns(pe, work)


_INS = ["L0_attn_input", "L0_attn_Wq", "L0_attn_Wk", "L0_attn_Wv", "L0_attn_Wo", "L0_attn_bo", "L0_ffn_wqkv",
        "L0_ffn_q_scale", "L0_ffn_k_scale", "L0_ffn_wo", "L0_ffn_ln_g", "L0_ffn_ln_b", "L0_ffn_w1", "L0_ffn_b1",
        "L0_ffn_w2", "L0_ffn_b2"]


def kernel(**inputs):
    import numpy as _np
    import concourse.bacc as _bacc
    from concourse import mybir as _mybir
    from concourse.bass_utils import run_bass_kernel_spmd as _run

    nc = _bacc.Bacc("TRN2", target_bir_lowering=False, num_devices=1)
    arrays, args = {}, []
    for name in _INS:
        a = _np.ascontiguousarray(inputs[name])
        arrays[f"in_{name}"] = a
        args.append(nc.dram_tensor(f"in_{name}", a.shape, _mybir.dt.from_np(a.dtype), kind="ExternalInput").ap())
    _, c = shape_constants()
    arrays["in_constants"] = c
    args.append(nc.dram_tensor("in_constants", c.shape, _mybir.dt.float32, kind="ExternalInput").ap())
    out = nc.dram_tensor("out_0", inputs["L0_attn_input"].shape, _mybir.dt.float32, kind="ExternalOutput")
    program(nc, *args, out.ap())
    r = _run(nc, [arrays], core_ids=[0])
    return _np.asarray(r.results[0]["out_0"])
```
